# Optimizing a Trainium2 kernel written in Bass

```python
import numpy as np
import jax
import jax.numpy as jnp

def _softmax(x, axis=-1):
    return jax.nn.softmax(x, axis=axis)

def _gelu(x):
    return jax.nn.gelu(x, approximate=True)

def _silu(x):
    return jax.nn.silu(x)

def _sigmoid(x):
    return jax.nn.sigmoid(x)

def _layernorm(x, axis=-1, eps=1e-05):
    m = jnp.mean(x, axis=axis, keepdims=True)
    v = jnp.var(x, axis=axis, keepdims=True)
    return (x - m) / jnp.sqrt(v + eps)

def _scatter_add(tgt, idx, src, axis=0):
    return tgt.at[idx].add(src)

def _segment_sum(src, seg, n):
    return jax.ops.segment_sum(src, seg, n)
kernel_name = 'mk_adj_ffn_d1_adj_r2_80bec1'

def setup_inputs(seed: int=0):
    np.random.seed(seed)
    _w = jnp.asarray

    def _rec_inputs():
        import jax
        import jax.numpy as jnp
        _gk = jax.random.key(seed)
        x = 0.5 + 0.2887 * jax.random.normal(jax.random.fold_in(_gk, 1), (2048, 512), jnp.float32)
        _a = jax.random.bernoulli(jax.random.fold_in(_gk, 2), 0.00390625, (2048, 2048))
        _a = jnp.logical_or(_a, jnp.swapaxes(_a, -1, -2))
        _a = jnp.logical_or(_a, jnp.eye(2048, dtype=bool))
        _af = _a.astype(jnp.float32)
        _af = _af * jax.random.uniform(jax.random.fold_in(_gk, 3), (2048, 2048), jnp.float32, 0.05, 1)
        adj = _af
        return (x, adj)
    x, adj = _rec_inputs()

    def _L0_gnn_setup():
        import jax, jax.numpy as jnp
        import numpy as np
        NBITS = 4
        N_NODES = 4096
        IN_F = 512
        OUT_F = 512

        def _act_quant(x, alpha, b):
            n = float(2 ** b - 1)
            xd = x / alpha
            xc = jnp.minimum(xd, 1.0)
            xq = jnp.round(xc * n) / n
            return xq * alpha

        def _weight_quant(w, alpha, b):
            n = float(2 ** b - 1)
            wd = w / alpha
            wc = jnp.clip(wd, -1.0, 1.0)
            wq = jnp.round(jnp.abs(wc) * n) / n * jnp.sign(wc)
            return wq * alpha
        key = jax.random.key(seed)
        k1, k2, k3 = jax.random.split(key, 3)
        stdv = 1.0 / np.sqrt(OUT_F)
        inp = {'input': jax.random.uniform(k1, (N_NODES, IN_F), dtype=jnp.float32), 'adj': jax.random.uniform(k2, (N_NODES, N_NODES), dtype=jnp.float32), 'adj_scaling_factor': jnp.float32(2.0), 'weight': jax.random.uniform(k3, (IN_F, OUT_F), minval=-stdv, maxval=stdv, dtype=jnp.float32), 'wgt_alpha': jnp.float32(3.0), 'act_alpha': jnp.float32(1.0), 'act_alpha2': jnp.float32(1.0)}
        return inp
    _L0_gnn_all = _L0_gnn_setup()
    _L0_gnn_in = {k: v for k, v in _L0_gnn_all.items() if k in ('adj_scaling_factor', 'weight', 'wgt_alpha', 'act_alpha', 'act_alpha2')}
    del _L0_gnn_all

    def _L0_ffn_setup():
        import jax, jax.numpy as jnp
        import numpy as np
        IN_DIM = 512
        HIDDEN = 512
        OUT_DIM = 512
        NUM_EXPERTS = 16
        TOP_K = 2
        ROUTER_TEMP = 1.0
        LN_EPS = 1e-05

        def _layernorm(h, g, b):
            mu = jnp.mean(h, axis=-1, keepdims=True)
            var = jnp.mean(jnp.square(h - mu), axis=-1, keepdims=True)
            return (h - mu) * jax.lax.rsqrt(var + LN_EPS) * g + b
        key = jax.random.key(seed)
        ks = jax.random.split(key, 8)
        s_in = 1.0 / np.sqrt(IN_DIM)
        s_h = 1.0 / np.sqrt(HIDDEN)
        x = jax.random.normal(ks[0], (4, 1024, IN_DIM), dtype=jnp.float32)
        Wr = jax.random.uniform(ks[1], (IN_DIM, NUM_EXPERTS), jnp.float32, -s_in, s_in)
        br = jax.random.uniform(ks[2], (NUM_EXPERTS,), jnp.float32, -s_in, s_in)
        W1 = jax.random.uniform(ks[3], (NUM_EXPERTS, IN_DIM, HIDDEN), jnp.float32, -s_in, s_in)
        b1 = jax.random.uniform(ks[4], (NUM_EXPERTS, HIDDEN), jnp.float32, -s_in, s_in)
        g1 = jnp.ones((NUM_EXPERTS, HIDDEN), jnp.float32)
        be1 = jnp.zeros((NUM_EXPERTS, HIDDEN), jnp.float32)
        W2 = jax.random.uniform(ks[5], (NUM_EXPERTS, HIDDEN, OUT_DIM), jnp.float32, -s_h, s_h)
        b2 = jax.random.uniform(ks[6], (NUM_EXPERTS, OUT_DIM), jnp.float32, -s_h, s_h)
        return {'x': x, 'Wr': Wr, 'br': br, 'W1': W1, 'b1': b1, 'g1': g1, 'be1': be1, 'W2': W2, 'b2': b2}
    _L0_ffn_all = _L0_ffn_setup()
    _L0_ffn_in = {k: v for k, v in _L0_ffn_all.items() if k in ('Wr', 'br', 'W1', 'b1', 'g1', 'be1', 'W2', 'b2')}
    del _L0_ffn_all
    return {'x': x, 'adj': adj, 'L0_gnn_adj_scaling_factor': _L0_gnn_in['adj_scaling_factor'], 'L0_gnn_weight': _L0_gnn_in['weight'], 'L0_gnn_wgt_alpha': _L0_gnn_in['wgt_alpha'], 'L0_gnn_act_alpha': _L0_gnn_in['act_alpha'], 'L0_gnn_act_alpha2': _L0_gnn_in['act_alpha2'], 'L0_ffn_Wr': _L0_ffn_in['Wr'], 'L0_ffn_br': _L0_ffn_in['br'], 'L0_ffn_W1': _L0_ffn_in['W1'], 'L0_ffn_b1': _L0_ffn_in['b1'], 'L0_ffn_g1': _L0_ffn_in['g1'], 'L0_ffn_be1': _L0_ffn_in['be1'], 'L0_ffn_W2': _L0_ffn_in['W2'], 'L0_ffn_b2': _L0_ffn_in['b2']}

def reference(x, adj, L0_gnn_adj_scaling_factor, L0_gnn_weight, L0_gnn_wgt_alpha, L0_gnn_act_alpha, L0_gnn_act_alpha2, L0_ffn_Wr, L0_ffn_br, L0_ffn_W1, L0_ffn_b1, L0_ffn_g1, L0_ffn_be1, L0_ffn_W2, L0_ffn_b2):
    import jax
    import jax.numpy as jnp

    def _L0_gnn_ref(input, adj, adj_scaling_factor, weight, wgt_alpha, act_alpha, act_alpha2):
        import jax, jax.numpy as jnp
        import numpy as np
        NBITS = 4
        N_NODES = 4096
        IN_F = 512
        OUT_F = 512

        def _act_quant(x, alpha, b):
            n = float(2 ** b - 1)
            xd = x / alpha
            xc = jnp.minimum(xd, 1.0)
            xq = jnp.round(xc * n) / n
            return xq * alpha

        def _weight_quant(w, alpha, b):
            n = float(2 ** b - 1)
            wd = w / alpha
            wc = jnp.clip(wd, -1.0, 1.0)
            wq = jnp.round(jnp.abs(wc) * n) / n * jnp.sign(wc)
            return wq * alpha
        bit = NBITS
        wb = bit - 1
        mean = jax.lax.stop_gradient(jnp.mean(weight))
        std = jax.lax.stop_gradient(jnp.std(weight, ddof=1))
        w_norm = (weight - mean) / std
        weight_q = _weight_quant(w_norm, wgt_alpha, wb)
        x = _act_quant(input, act_alpha, bit)
        wgt_delta = wgt_alpha / (2 ** (bit - 1) - 1)
        act_delta = act_alpha / (2 ** bit - 1)
        support = jnp.matmul(x / act_delta, weight_q / wgt_delta)
        support = support * act_delta * wgt_delta
        support = jax.nn.relu(support)
        support_q = _act_quant(support, act_alpha2, bit)
        support_delta = act_alpha2 / (2 ** bit - 1)
        output = jnp.matmul(adj / adj_scaling_factor, support_q / support_delta)
        return output * adj_scaling_factor * support_delta

    def _L0_ffn_ref(x, Wr, br, W1, b1, g1, be1, W2, b2):
        import jax, jax.numpy as jnp
        import numpy as np
        IN_DIM = 512
        HIDDEN = 512
        OUT_DIM = 512
        NUM_EXPERTS = 16
        TOP_K = 2
        ROUTER_TEMP = 1.0
        LN_EPS = 1e-05

        def _layernorm(h, g, b):
            mu = jnp.mean(h, axis=-1, keepdims=True)
            var = jnp.mean(jnp.square(h - mu), axis=-1, keepdims=True)
            return (h - mu) * jax.lax.rsqrt(var + LN_EPS) * g + b
        orig_shape = x.shape[:-1]
        x_flat = x.reshape(-1, x.shape[-1])
        logits = (x_flat @ Wr + br) / max(ROUTER_TEMP, 1e-06)
        probs = jax.nn.softmax(logits, axis=-1)
        topk_w, topk_idx = jax.lax.top_k(probs, TOP_K)
        topk_w = topk_w / jnp.clip(jnp.sum(topk_w, axis=-1, keepdims=True), 1e-09)
        h = jnp.einsum('nc,ech->neh', x_flat, W1) + b1
        h = _layernorm(h, g1, be1)
        h = jax.nn.gelu(h, approximate=False)
        expert_out = jnp.einsum('neh,eho->neo', h, W2) + b2
        sel = jnp.take_along_axis(expert_out, topk_idx[:, :, None], axis=1)
        y_flat = jnp.sum(sel * topk_w[:, :, None], axis=1)
        return y_flat.reshape(*orig_shape, y_flat.shape[-1])
    x = x + _L0_gnn_ref(_layernorm(x, axis=-1), adj, L0_gnn_adj_scaling_factor, L0_gnn_weight, L0_gnn_wgt_alpha, L0_gnn_act_alpha, L0_gnn_act_alpha2)
    x = x + _L0_ffn_ref(_layernorm(x, axis=-1)[None], L0_ffn_Wr, L0_ffn_br, L0_ffn_W1, L0_ffn_b1, L0_ffn_g1, L0_ffn_be1, L0_ffn_W2, L0_ffn_b2)[0]
    return x

_drawn_inputs = setup_inputs


def setup_inputs(seed=0):
    import zlib

    import numpy as np

    out = dict(_drawn_inputs(seed))
    spreads = {'L0_ffn_g1': (1.0, 0.6), 'L0_ffn_be1': (0.0, 0.8)}
    factors = {'L0_ffn_br': 5.37, 'L0_ffn_b1': 8.0, 'L0_ffn_b2': 8.0}
    for name, (base, spread) in spreads.items():
        noise = np.random.default_rng([zlib.crc32(name.encode()), seed]).standard_normal(out[name].shape)
        drawn = base * np.exp(spread * noise) if base else spread * noise
        out[name] = jnp.asarray(drawn.astype(out[name].dtype))
    for name, factor in factors.items():
        out[name] = (out[name] * factor).astype(out[name].dtype)
    return out
```

```python
from contextlib import ExitStack

import numpy as np

import concourse.bass as bass
from concourse import mybir

ALU = mybir.AluOpType
ACT = mybir.ActivationFunctionType
F32 = mybir.dt.float32
F32R = mybir.dt.float32r
I32 = mybir.dt.int32
AX_X = mybir.AxisListType.X

P = 128
N = 2048
D = 512
E = 16
T = N // P
C = D // P
TOP = 2
SLOTS = (TOP * N - E) // P + E
SLOTS += SLOTS % 2
TAB = SLOTS + 4
QUARTERS = 4
TQ = T // QUARTERS
STEPS = T // 2
LN_EPS = 1e-5
MAGIC = 1.5 * 2.0 ** 23
N_ACT = 15.0
N_WGT = 7.0

_WIDTHS = [("ident", P), ("tri", P), ("ones", P), ("iota_row", P), ("iota_slot", TAB), ("iota_e", E),
           ("full_tiles", E), ("token", T), ("is_bias1", 1), ("is_bias2", 1), ("dump_row", 1),
           ("scan_keep", E * T), ("neg_half", 1), ("minus_one", 1)]
COLS, _at = {}, 0
for _name, _w in _WIDTHS:
    COLS[_name] = (_at, _at + _w)
    _at += _w
CONSTS = _at


def constants():
    k = np.zeros((P, CONSTS), np.float32)
    p = np.arange(P)

    def put(name, v):
        a, b = COLS[name]
        k[:, a:b] = v

    put("ident", np.eye(P))
    put("tri", p[:, None] < p[None, :])
    put("ones", 1.0)
    put("iota_row", p[None, :])
    put("iota_slot", np.arange(TAB)[None, :])
    put("iota_e", np.arange(E)[None, :])
    put("full_tiles", P * np.arange(E)[None, :])
    put("token", P * np.arange(T)[None, :] + p[:, None])
    put("is_bias1", np.where(p < 64, p % 32, 1000)[:, None])
    put("is_bias2", np.where(p >= 64, p % 32, 1000)[:, None])
    put("dump_row", (N + p)[:, None])
    put("scan_keep", np.tile((np.arange(T) > 0).astype(np.float32), E)[None, :])
    put("neg_half", -0.5)
    put("minus_one", -1.0)
    return k


class Chain:

    def __init__(self, eng, sem):
        self.eng, self.sem = eng, sem
        self.base, self.n, self.i, self.per = 0, 0, None, 0

    def link(self, ins):
        self.n += 1
        ins.then_inc(self.sem, 1)
        at = self.base + self.n
        self.eng.wait_ge(self.sem, at if self.i is None else self.i * self.per + at)

    def enter(self, i, per):
        self.base, self.n, self.i, self.per = self.base + self.n, 0, i, per

    def leave(self, trips):
        assert self.n == self.per, (self.n, self.per)
        self.base, self.n, self.i = self.base + trips * self.per, 0, None


def gnn_moe_program(nc, x, adj_t, gnn_w, scalars, wr, br, w1, b1, g1, be1, w2, b2, consts, xn_rows, out):
    with ExitStack() as ctx:
        usable = nc.sbuf_usable_end
        first = (nc.sbuf_base + 31) // 32 * 32
        where = [first]

        def place(name, shape, dt):
            size = int(np.prod(shape[1:])) * 4
            t = nc.alloc_sbuf_tensor_at(name, shape, dt, offset=where[0])
            where[0] += (size + 31) // 32 * 32
            assert where[0] <= usable, (name, where[0], usable)
            return t

        def sem(name):
            return ctx.enter_context(nc.semaphore(name))

        k_sb = place("k_sb", [P, CONSTS], F32)
        sc = place("sc", [P, 4], F32)
        g1_sb = place("g1_sb", [P, E * C], F32)
        be1_sb = place("be1_sb", [P, E * C], F32)
        br_sb = place("br_sb", [P, E], F32)
        wr_sb = place("wr_sb", [P, C * E], F32)
        bias_sb = place("bias_sb", [P, D], F32R)
        w_raw = place("w_raw", [P, 2, 2, C * D], F32)
        logits = place("logits", [P, T, E], F32)
        small = place("small", [P, 64], F32)
        stats = place("stats", [P, 4, 6], F32)
        mv = place("mv", [P, T, 2], F32)
        rstd = place("rstd", [P, T, 2], F32)
        tok_i = place("tok_i", [P, TAB], I32)
        scat_i = place("scat_i", [P, TAB], I32)
        gate = place("gate", [P, TAB], F32)
        sel1_col = place("sel1_col", [P, TAB], F32)
        sel2_col = place("sel2_col", [P, TAB], F32)
        slot_e = place("slot_e", [P, TAB], I32)
        prep1 = place("prep1", [P, TAB], I32)
        prep2 = place("prep2", [P, TAB], I32)
        end_fixed = where[0]

        sup = place("sup", [P, T, D], F32R)
        adj_raw = place("adj_raw", [P, 2, 2, D], F32)
        adj_hi = place("adj_hi", [P, 2, 2, D], F32R)
        adj_lo = place("adj_lo", [P, 2, 2, D], F32R)
        xq = place("xq", [P, 2, D], F32)
        xq_hi = place("xq_hi", [P, 2, D], F32R)
        xq_lo = place("xq_lo", [P, 2, D], F32R)
        end_adj = where[0]
        w_int = place("w_int", [P, C * D], F32R)
        x_sb = place("x_sb", [P, T, D], F32)
        xn = place("xn", [P, 2, D], F32)
        xn_t = place("xn_t", [P, 2, D], F32)
        gw_raw = place("gw_raw", [P, C * D], F32)
        relu_sb = place("relu_sb", [P, 2, D], F32)
        rt = place("rt", [P, 14, E * T], F32)
        rv = place("rv", [P, 16, 32], F32)
        b_raw = place("b_raw", [P, D], F32)
        b_hi = place("b_hi", [P, D], F32R)
        end_gnn = where[0]

        where[0] = end_fixed
        w_hi = place("w_hi", [P, 2, 2 * C * D], F32R)
        w_lo = place("w_lo", [P, 2, 2 * C * D], F32R)
        end_w = where[0]
        where[0] = max(end_w, end_adj)
        ffn0 = where[0]
        xg = place("xg", [P, 2, D], F32)
        xt_hi = place("xt_hi", [P, 2, D], F32R)
        xt_lo = place("xt_lo", [P, 2, D], F32R)
        h_hat = place("h_hat", [P, 2, D], F32)
        g_sb = place("g_sb", [P, 2, D], F32)
        gt_hi = place("gt_hi", [P, 2, D], F32R)
        gt_lo = place("gt_lo", [P, 2, D], F32R)
        y_sb = place("y_sb", [P, D], F32)
        sel1 = place("sel1", [P, 2, P], F32R)
        sel2 = place("sel2", [P, 2, P], F32R)
        idx_g = place("idx_g", [P, 2], I32)
        idx_s = place("idx_s", [P, 2], I32)
        h_stats = place("h_stats", [P, 2, 6], F32)
        h_mv = place("h_mv", [P, 2, 2], F32)
        h_rs = place("h_rs", [P, 2, 4], F32)
        hit_row = place("hit_row", [P, TOP * T, P], F32R)
        assert where[0] <= end_gnn
        where[0] = ffn0
        hit_slot = place("hit_slot", [P, TOP * T * TAB], F32)
        hit_val = place("hit_val", [P, 4, TOP * T * TAB // 2], F32R)

        ps = ctx.enter_context(nc.psum_tensor("ps", [P, 8, D], F32))

        def const(name):
            a, b = COLS[name]
            return k_sb[:, a:b]

        consts_in = sem("consts_in")
        gw_in = sem("gw_in")
        x_in = [sem(f"x_in{i}") for i in range(4)]
        adj_in = [sem(f"adj_in{i}") for i in range(2)]
        dve_own = sem("dve_own")
        pool_own = sem("pool_own")
        pool_turn = sem("pool_turn")
        dve_turn = sem("dve_turn")
        w_means = sem("w_means")
        w_sums = sem("w_sums")
        w_var = sem("w_var")
        w_rstd = sem("w_rstd")
        w_ready = sem("w_ready")
        x_var = sem("x_var")
        x_rstd = sem("x_rstd")
        xq_ready = sem("xq_ready")
        xq_t = sem("xq_t")
        xq_hi_ok = sem("xq_hi_ok")
        xq_lo_ok = sem("xq_lo_ok")
        sup_mm = sem("sup_mm")
        relu_ok = sem("relu_ok")
        sup_ok = sem("sup_ok")
        adj_hi_ok = sem("adj_hi_ok")
        adj_lo_ok = sem("adj_lo_ok")
        adj_mm = sem("adj_mm")
        acc_read = sem("acc_read")
        mid_ok = sem("mid_ok")
        mid_rstd = sem("mid_rstd")
        xn_ok = sem("xn_ok")
        xn_tp = sem("xn_tp")
        xn_t_ok = sem("xn_t_ok")
        router_mm = sem("router_mm")
        logits_ok = sem("logits_ok")
        mid_out = [sem(f"mid_out{i}") for i in range(2)]
        bias_in = sem("bias_in")
        bias_ok = sem("bias_ok")
        exp_in = sem("exp_in")
        exp_ok = sem("exp_ok")
        picked = sem("picked")
        ranks = sem("ranks")
        hits_ok = sem("hits_ok")
        table_mm = sem("table_mm")
        table_ok = sem("table_ok")
        raw_in = [sem(f"raw{n}_in") for n in (1, 2)]
        split_hi = [sem(f"split{n}_hi") for n in (1, 2)]
        split_lo = [sem(f"split{n}_lo") for n in (1, 2)]
        gathered = [sem(f"gathered{i}") for i in range(2)]
        x_tp = sem("x_tp")
        x_hi_ok = sem("x_hi_ok")
        x_lo_ok = sem("x_lo_ok")
        sel_ok = sem("sel_ok")
        mm1 = sem("mm1")
        h_var = sem("h_var")
        h_rstd = sem("h_rstd")
        h_hat_ok = sem("h_hat_ok")
        h_tp = sem("h_tp")
        gelu_ok = sem("gelu_ok")
        g_hi_ok = sem("g_hi_ok")
        g_lo_ok = sem("g_lo_ok")
        mm2 = sem("mm2")
        y_ok = sem("y_ok")
        scattered = sem("scattered")

        block = ctx.enter_context(nc.Block())

        def acc_bank(q, i):
            return ps[:, 4 * (q % 2) + i, :]

        def side_bank(q, i):
            return ps[:, 4 * (1 - q % 2) + i, :]

        def xt_ps(par):
            return ps[:, par, :]

        def h_ps(par):
            return ps[:, 2 + par, :]

        def ht_ps(par):
            return ps[:, 4 + par, :]

        y_ps = ps[:, 6, :]
        MID = 3

        @block.sync
        def _(sp):
            sp.dma_start(gw_raw[:, :], gnn_w).then_inc(gw_in, 16)
            for i in range(4):
                sp.dma_start(x_sb[:, 4 * i:4 * i + 4, :],
                             x[4 * i * P:(4 * i + 4) * P, :].rearrange("(t p) d -> p t d", p=P)).then_inc(x_in[i], 16)
            view = adj_t.rearrange("(s k p) n -> p s k n", p=P, k=2)

            def load_adj(q, m, par):
                return sp.dma_start(adj_raw[:, par, :, :],
                                    view[:, m:m + 1, :, q * D:(q + 1) * D].rearrange("p s k n -> p (s k) n")
                                    if isinstance(m, int) else
                                    view[:, bass.ds(m, 1), :, q * D:(q + 1) * D].rearrange("p s k n -> p (s k) n")
                                    ).then_inc(adj_in[par], 16)

            for q in range(QUARTERS):
                for par in range(2):
                    if q:
                        sp.wait_ge(adj_lo_ok, STEPS * q - 1 + par)
                    load_adj(q, par, par)
                with sp.Fori(1, STEPS // 2) as j:
                    for par in range(2):
                        sp.wait_ge(adj_lo_ok, j * 2 + (STEPS * q - 1 + par))
                        load_adj(q, j * 2 + par, par)
            w_dram = (w1, w2)
            for e in range(2):
                for n in range(2):
                    if e:
                        sp.wait_ge(raw_in[n], 16)
                    sp.dma_start(w_raw[:, n, e, :], w_dram[n][e * P:(e + 1) * P, :]).then_inc(raw_in[n], 16)
            with sp.Fori(1, E // 2) as j:
                for par in range(2):
                    for n in range(2):
                        sp.wait_ge(raw_in[n], j * 32 + 16 * par)
                        sp.wait_ge(split_lo[n], j * 2 + (par - 1))
                        sp.dma_start(w_raw[:, n, par, :],
                                     w_dram[n][bass.ds(j * 2 * P + par * P, P), :]).then_inc(raw_in[n], 16)

        @block.gpsimd
        def _(pool):
            own = Chain(pool, pool_own)
            pool.dma_start(k_sb[:, :], consts).then_inc(consts_in, 16)
            pool.dma_start(sc[:, :], scalars).then_inc(consts_in, 16)
            pool.dma_start(g1_sb[:, :], g1).then_inc(consts_in, 16)
            pool.dma_start(be1_sb[:, :], be1).then_inc(consts_in, 16)
            pool.dma_start(br_sb[:, :], br).then_inc(consts_in, 16)
            pool.dma_start(wr_sb[:, :], wr).then_inc(consts_in, 16)
            own.link(pool.memset(b_raw[:, :], 0.0))
            for base, b in ((0, b1), (32, b1), (64, b2), (96, b2)):
                pool.dma_start(b_raw[base:base + E, :], b).then_inc(bias_in, 16)
            neg_half = const("neg_half")
            pool.wait_ge(consts_in, 96)
            pool.dma_start(out[N:N + P, :], k_sb[:, 0:D]).then_inc(scattered, 16)
            pool.wait_ge(w_var, 1)
            pool.tensor_tensor(small[:, 13:14], small[:, 12:13], neg_half, ALU.pow).then_inc(w_rstd, 1)
            pool.wait_ge(x_var, 1)
            pool.tensor_tensor(rstd[:, :, 0], rstd[:, :, 1], neg_half.to_broadcast([P, T]), ALU.pow).then_inc(x_rstd, 1)

            for t in range(T):
                pool.wait_ge(mid_ok, t + 1)
                own.link(pool.tensor_scalar(rstd[:, t, 1:2], mv[:, t, 1:2], LN_EPS, None, ALU.add))
                own.link(pool.tensor_tensor(rstd[:, t, 0:1], rstd[:, t, 1:2], neg_half, ALU.pow))
                own.link(pool.tensor_tensor(rstd[:, t, 1:2], mv[:, t, 0:1], rstd[:, t, 0:1], ALU.mult))
                pool.tensor_scalar(rstd[:, t, 1:2], rstd[:, t, 1:2], -1.0, None, ALU.mult).then_inc(mid_rstd, 1)

            def select(dst, par, col, s):
                return pool.tensor_copy(dst[:, par, :], col[:, bass.ds(s, 1)].to_broadcast([P, P]))

            def gather(par):
                return pool.indirect_dma_start(
                    xg[:, par, :], None, xn_rows,
                    bass.IndirectOffsetOnAxis(ap=idx_g[:, par:par + 1], axis=0)).then_inc(gathered[par], 16)

            def slot_rstd(par):
                own.link(pool.tensor_scalar(h_rs[:, par, 2:3], h_mv[:, par, 1:2], LN_EPS, None, ALU.add))
                own.link(pool.tensor_tensor(h_rs[:, par, 0:1], h_rs[:, par, 2:3], neg_half, ALU.pow))
                own.link(pool.tensor_tensor(h_rs[:, par, 3:4], h_mv[:, par, 0:1], h_rs[:, par, 0:1], ALU.mult))
                pool.tensor_tensor(h_rs[:, par, 1:2], h_rs[:, par, 3:4], const("minus_one"), ALU.mult).then_inc(h_rstd, 1)

            pool.wait_ge(table_ok, 1)
            for i in range(2):
                pool.wait_ge(mid_out[i], 16 * T)
            pool.wait_ge(scattered, 16)
            for s in range(4):
                if s >= 2:
                    pool.wait_ge(gathered[s % 2], 16)
                    pool.wait_ge(x_tp, s - 1)
                own.link(pool.tensor_copy(idx_g[:, s % 2:s % 2 + 1], tok_i[:, s:s + 1]))
                gather(s % 2)
                if s == 1:
                    select(sel1, 0, sel1_col, 0).then_inc(sel_ok, 1)
                    select(sel1, 1, sel1_col, 1).then_inc(sel_ok, 1)
                    select(sel2, 0, sel2_col, 0).then_inc(sel_ok, 1)
            pool.wait_ge(h_var, 1)
            slot_rstd(0)

            with pool.Fori(0, SLOTS // 2) as j:
                own.enter(j, 2 * 5)
                for par in range(2):
                    s = j * 2 + par
                    pool.wait_ge(x_tp, s + 3)
                    pool.sem_inc(pool_turn, 1)
                    select(sel1, par, sel1_col, s + 2).then_inc(sel_ok, 1)
                    select(sel2, 1 - par, sel2_col, s + 1).then_inc(sel_ok, 1)
                    own.link(pool.tensor_copy(idx_g[:, par:par + 1], tok_i[:, bass.ds(s + 4, 1)]))
                    pool.sem_inc(pool_turn, 1)
                    gather(par)
                    pool.wait_ge(h_var, s + 2)
                    pool.sem_inc(pool_turn, 1)
                    slot_rstd(1 - par)
                    own.link(pool.tensor_copy(idx_s[:, par:par + 1], scat_i[:, bass.ds(s, 1)]))
                    pool.wait_ge(y_ok, s + 2)
                    pool.sem_inc(pool_turn, 1)
                    pool.indirect_dma_start(
                        out, bass.IndirectOffsetOnAxis(ap=idx_s[:, par:par + 1], axis=0),
                        y_sb[:, :], None, compute_op=ALU.add).then_inc(scattered, 16)
                own.leave(SLOTS // 2)
            pool.wait_ge(scattered, 16 * SLOTS + 16)
            for par in range(2):
                pool.wait_ge(gathered[par], 16 * (SLOTS // 2 + 2))

        @block.scalar
        def _(act):
            def hi_step(par, arrived, before):
                act.wait_ge(adj_in[par], arrived)
                if before is not None:
                    act.wait_ge(adj_mm, before + 1)
                act.activation(adj_hi[:, par, :, :], adj_raw[:, par, :, :], ACT.Copy, scale=small[:, 0:1]).then_inc(adj_hi_ok, 1)

            def g_hi(t, par):
                act.wait_ge(xq_t, t + 1)
                act.activation(xq_hi[:, par, :], side_bank(0, par), ACT.Copy, bias=-MAGIC).then_inc(xq_hi_ok, 1)

            def g_relu(t, par):
                act.wait_ge(sup_mm, t + 1)
                act.activation(relu_sb[:, par, :], side_bank(0, 2 + par), ACT.Relu, scale=small[:, 5:6]).then_inc(relu_ok, 1)

            def finish_xn(t):
                act.wait_ge(mid_rstd, t + 1)
                if t >= 2:
                    act.wait_ge(xn_tp, t - 1)
                    act.wait_ge(mid_out[t % 2], 32 * (t // 2))
                act.activation(xn[:, t % 2, :], x_sb[:, t, :], ACT.Identity, scale=rstd[:, t, 0:1],
                               bias=rstd[:, t, 1:2]).then_inc(xn_ok, 1)
                act.dma_start(out[t * P:(t + 1) * P, :], x_sb[:, t, :]).then_inc(mid_out[t % 2], 16)
                act.wait_ge(xn_ok, t + 1)
                act.dma_start(xn_rows[t * P:(t + 1) * P, :], xn[:, t % 2, :]).then_inc(mid_out[t % 2], 16)

            def finish_t(t):
                act.wait_ge(xn_tp, t + 1)
                act.activation(xn_t[:, t % 2, :], side_bank(t // TQ + 1, t % 2), ACT.Copy).then_inc(xn_t_ok, 1)

            act.wait_ge(w_ready, 1)
            g_hi(0, 0)
            g_hi(1, 1)
            g_relu(0, 0)
            hi_step(0, 16, None)
            g_hi(2, 0)
            g_relu(1, 1)
            with act.Fori(0, MID) as j:
                for half in range(2):
                    par = 1 - half
                    g_hi(j * 4 + (2 * half + 3), 1)
                    g_relu(j * 4 + (2 * half + 2), 0)
                    hi_step(par, j * 16 + 16 * (1 + half), j * 2 + half)
                    g_hi(j * 4 + (2 * half + 4), 0)
                    g_relu(j * 4 + (2 * half + 3), 1)
            g_hi(T - 1, 1)
            g_relu(T - 2, 0)
            hi_step(1, 16 * (STEPS // 2), STEPS - 2)
            g_relu(T - 1, 1)
            for q in range(1, QUARTERS):
                t0 = TQ * (q - 1)
                in0 = 16 * (STEPS // 2) * q
                hi_step(0, in0 + 16, STEPS * q - 1)
                for jj in range(MID):
                    hi_step(1, in0 + 16 * (jj + 1), STEPS * q + 2 * jj)
                    finish_xn(t0 + jj)
                    hi_step(0, in0 + 16 * (jj + 2), STEPS * q + 2 * jj + 1)
                    finish_t(t0 + jj)
                hi_step(1, in0 + 16 * (STEPS // 2), STEPS * (q + 1) - 2)
                finish_xn(t0 + MID)
                finish_t(t0 + MID)
            for t in range(T - TQ, T):
                finish_xn(t)
                finish_t(t)

            def split(n, par, arrived):
                act.wait_ge(raw_in[n], arrived)
                act.activation(w_hi[:, n, par * C * D:(par + 1) * C * D], w_raw[:, n, par, :], ACT.Copy).then_inc(split_hi[n], 1)

            act.wait_ge(adj_mm, STEPS * QUARTERS + 1)
            split(0, 0, 16)
            split(0, 1, 32)
            split(1, 0, 16)
            act.wait_ge(exp_in, 1)
            act.activation(rt[:, 1, :], rt[:, 0, :], ACT.Exp).then_inc(exp_ok, 1)

            def slot_x_hi(s, par):
                act.wait_ge(x_tp, s + 1)
                act.activation(xt_hi[:, par, :], xt_ps(par), ACT.Copy).then_inc(x_hi_ok, 1)

            def slot_h_hat(s, par):
                act.wait_ge(h_rstd, s + 1)
                act.activation(h_hat[:, par, :], h_ps(par), ACT.Identity, scale=h_rs[:, par, 0:1],
                               bias=h_rs[:, par, 1:2]).then_inc(h_hat_ok, 1)

            act.wait_ge(table_ok, 1)
            slot_x_hi(0, 0)
            slot_x_hi(1, 1)
            slot_h_hat(0, 0)
            with act.Fori(0, SLOTS // 2) as j:
                for par in range(2):
                    s = j * 2 + par
                    e_s = act.value_load(slot_e[0:1, bass.ds(s, 1)], min_val=0, max_val=E - 1)
                    e_n = act.value_load(slot_e[0:1, bass.ds(s + 1, 1)], min_val=0, max_val=E - 1)
                    do1 = act.value_load(prep1[0:1, bass.ds(s, 1)], min_val=0, max_val=1)
                    do2 = act.value_load(prep2[0:1, bass.ds(s, 1)], min_val=0, max_val=1)
                    act.wait_ge(h_tp, s + 1)
                    for c in range(C):
                        ins = act.activation(g_sb[:, par, c * P:(c + 1) * P], ht_ps(par)[:, c * P:(c + 1) * P], ACT.Gelu,
                                             scale=g1_sb[:, bass.ds(e_s * C + c, 1)],
                                             bias=be1_sb[:, bass.ds(e_s * C + c, 1)])
                    ins.then_inc(gelu_ok, 1)
                    act.wait_ge(gelu_ok, s + 1)
                    act.activation(gt_hi[:, par, :], g_sb[:, par, :], ACT.Copy).then_inc(g_hi_ok, 1)
                    slot_x_hi(s + 2, par)
                    with act.If(do1 == 1):
                        act.wait_ge(raw_in[0], e_n * 16 + 32)
                        act.activation(w_hi[:, 0, bass.ds(((e_n + 1) & 1) * (C * D), C * D)],
                                       w_raw[:, 0, :, :].rearrange("p a n -> p (a n)")[:, bass.ds(((e_n + 1) & 1) * (C * D), C * D)],
                                       ACT.Copy).then_inc(split_hi[0], 1)
                    with act.If(do2 == 1):
                        act.wait_ge(raw_in[1], e_s * 16 + 32)
                        act.activation(w_hi[:, 1, bass.ds(((e_s + 1) & 1) * (C * D), C * D)],
                                       w_raw[:, 1, :, :].rearrange("p a n -> p (a n)")[:, bass.ds(((e_s + 1) & 1) * (C * D), C * D)],
                                       ACT.Copy).then_inc(split_hi[1], 1)
                    slot_h_hat(s + 1, 1 - par)

        @block.vector
        def _(dve):
            own = Chain(dve, dve_own)
            link = own.link
            dve.wait_ge(consts_in, 96)

            link(dve.reciprocal(small[:, 0:4], sc[:, 0:4]))
            link(dve.tensor_scalar(small[:, 4:5], sc[:, 0:1], sc[:, 3:4], 1.0 / N_ACT, ALU.mult, ALU.mult))
            link(dve.tensor_scalar(small[:, 6:7], sc[:, 2:3], 1.0 / N_ACT, None, ALU.mult))
            link(dve.tensor_scalar(small[:, 7:8], sc[:, 1:2], 1.0 / N_WGT, None, ALU.mult))
            link(dve.tensor_tensor(small[:, 5:6], small[:, 6:7], small[:, 7:8], ALU.mult))

            dve.wait_ge(gw_in, 16)
            for c in range(C):
                ins = dve.bn_stats(stats[:, c, :], gw_raw[:, c * D:(c + 1) * D])
            link(ins)
            dve.bn_aggr(small[:, 8:10], stats[:, :, :].rearrange("p a b -> p (a b)")).then_inc(w_means, 1)
            dve.wait_ge(w_sums, 1)
            link(dve.tensor_scalar(small[:, 10:11], side_bank(0, 0)[:, 0:1], 1.0 / P, None, ALU.mult))
            link(dve.tensor_tensor(small[:, 11:12], small[:, 8:9], small[:, 10:11], ALU.subtract))
            link(dve.tensor_tensor(small[:, 14:15], small[:, 11:12], small[:, 11:12], ALU.mult))
            dve.tensor_tensor(small[:, 15:16], small[:, 14:15], small[:, 9:10], ALU.add).then_inc(w_means, 1)
            dve.wait_ge(w_sums, 2)
            dve.tensor_scalar(small[:, 12:13], side_bank(0, 1)[:, 0:1], D * D / (D * D - 1.0) / P, None,
                              ALU.mult).then_inc(w_var, 1)
            for t in range(T):
                if t % 4 == 0:
                    dve.wait_ge(x_in[t // 4], 16)
                link(dve.bn_stats(stats[:, t % 4, :], x_sb[:, t, :]))
                link(dve.bn_aggr(mv[:, t, :], stats[:, t % 4, :]))
            dve.tensor_scalar(rstd[:, :, 1], mv[:, :, 1], LN_EPS, None, ALU.add).then_inc(x_var, 1)
            dve.wait_ge(w_rstd, 1)
            link(dve.tensor_scalar(gw_raw[:, :], gw_raw[:, :], small[:, 10:11], small[:, 13:14], ALU.subtract, ALU.mult))
            link(dve.tensor_scalar(gw_raw[:, :], gw_raw[:, :], small[:, 1:2], 1.0, ALU.mult, ALU.min))
            link(dve.tensor_scalar(gw_raw[:, :], gw_raw[:, :], -1.0, N_WGT, ALU.max, ALU.mult))
            dve.tensor_scalar(w_int[:, :], gw_raw[:, :], MAGIC, MAGIC, ALU.add, ALU.subtract).then_inc(w_ready, 1)
            dve.wait_ge(x_rstd, 1)

            def x_tile(t):
                return x_sb[:, :, :].rearrange("p t d -> p (t d)")[:, bass.ds(t * D, D)]

            def sup_tile(t):
                return sup[:, :, :].rearrange("p t d -> p (t d)")[:, bass.ds(t * D, D)]

            def mean_of(t):
                return mv[:, :, :].rearrange("p t d -> p (t d)")[:, bass.ds(t * 2, 1)]

            def rstd_of(t):
                return rstd[:, :, :].rearrange("p t d -> p (t d)")[:, bass.ds(t * 2, 1)]

            def quantise_x(t, par):
                link(dve.tensor_scalar(xq[:, par, :], x_tile(t), mean_of(t), rstd_of(t), ALU.subtract, ALU.mult))
                link(dve.tensor_scalar(xq[:, par, :], xq[:, par, :], small[:, 2:3], 1.0, ALU.mult, ALU.min))
                dve.tensor_scalar(xq[:, par, :], xq[:, par, :], N_ACT, MAGIC, ALU.mult, ALU.add).then_inc(xq_ready, 1)

            def x_lo(t, par):
                dve.wait_ge(xq_hi_ok, t + 1)
                dve.scalar_tensor_tensor(xq_lo[:, par, :], side_bank(0, par), MAGIC, xq_hi[:, par, :].bitcast(F32),
                                         ALU.subtract, ALU.subtract).then_inc(xq_lo_ok, 1)

            def quantise_sup(t, par):
                dve.wait_ge(relu_ok, t + 1)
                link(dve.tensor_scalar(relu_sb[:, par, :], relu_sb[:, par, :], small[:, 3:4], 1.0, ALU.mult, ALU.min))
                link(dve.tensor_scalar(relu_sb[:, par, :], relu_sb[:, par, :], N_ACT, MAGIC, ALU.mult, ALU.add))
                dve.tensor_scalar(sup_tile(t), relu_sb[:, par, :], MAGIC, None, ALU.subtract).then_inc(sup_ok, 1)

            def lo_step(par, n):
                dve.wait_ge(adj_hi_ok, n)
                dve.scalar_tensor_tensor(adj_lo[:, par, :, :].rearrange("p a b -> p (a b)"),
                                         adj_raw[:, par, :, :].rearrange("p a b -> p (a b)"), small[:, 0:1],
                                         adj_hi[:, par, :, :].rearrange("p a b -> p (a b)").bitcast(F32),
                                         ALU.mult, ALU.subtract).then_inc(adj_lo_ok, 1)

            quantise_x(0, 0)
            quantise_x(1, 1)
            x_lo(0, 0)
            quantise_x(2, 0)
            x_lo(1, 1)
            quantise_sup(0, 0)
            lo_step(0, 1)
            quantise_x(3, 1)
            x_lo(2, 0)
            quantise_sup(1, 1)
            with dve.Fori(0, MID) as j:
                own.enter(j, 4 * 4)
                for half in range(2):
                    t = j * 4 + 2 * half
                    quantise_x(t + 4, 0)
                    x_lo(t + 3, 1)
                    quantise_sup(t + 2, 0)
                    lo_step(1 - half, j * 2 + (2 + half))
                    quantise_x(t + 5, 1)
                    x_lo(t + 4, 0)
                    quantise_sup(t + 3, 1)
                own.leave(MID)
            x_lo(T - 1, 1)
            quantise_sup(T - 2, 0)
            lo_step(1, STEPS)
            quantise_sup(T - 1, 1)

            def add_gnn(t):
                dve.scalar_tensor_tensor(x_sb[:, t, :], acc_bank(t // TQ, t % TQ), small[:, 4:5], x_sb[:, t, :],
                                         ALU.mult, ALU.add).then_inc(acc_read, 1)

            def statistics(t):
                dve.wait_ge(acc_read, t + 1)
                link(dve.bn_stats(stats[:, t % 4, :], x_sb[:, t, :]))
                dve.bn_aggr(mv[:, t, :], stats[:, t % 4, :]).then_inc(mid_ok, 1)

            def add_br(t):
                dve.wait_ge(router_mm, t + 1)
                dve.tensor_tensor(logits[:, t, :], side_bank(t // TQ + 1, 2 + t % 2)[:, 0:E], br_sb[:, :],
                                  ALU.add).then_inc(logits_ok, 1)

            for q in range(1, QUARTERS):
                t0 = TQ * (q - 1)
                lo_step(0, STEPS * q + 1)
                dve.wait_ge(adj_mm, STEPS * q + 1)
                for t in range(t0, t0 + TQ):
                    add_gnn(t)
                statistics(t0)
                for jj in range(MID):
                    lo_step(1, STEPS * q + 2 * jj + 2)
                    lo_step(0, STEPS * q + 2 * jj + 3)
                    statistics(t0 + jj + 1)
                    add_br(t0 + jj)
                lo_step(1, STEPS * (q + 1))
                add_br(t0 + MID)
            dve.wait_ge(adj_mm, STEPS * QUARTERS + 1)
            for t in range(T - TQ, T):
                add_gnn(t)
            for t in range(T - TQ, T):
                statistics(t)
            for t in range(T - TQ, T):
                add_br(t)
            dve.wait_ge(logits_ok, T)

            def split(n, par, ready):
                dve.wait_ge(split_hi[n], ready)
                dve.tensor_tensor(w_lo[:, n, par * C * D:(par + 1) * C * D], w_raw[:, n, par, :],
                                  w_hi[:, n, par * C * D:(par + 1) * C * D].bitcast(F32), ALU.subtract).then_inc(split_lo[n], 1)

            def te(i):
                return rt[:, i, :].rearrange("p (t e) -> p t e", e=E)

            def et(i):
                return rt[:, i, :].rearrange("p (e t) -> p e t", t=T)

            def over_e(v):
                return v.unsqueeze(2).to_broadcast([P, T, E])

            def over_t(v):
                return v.unsqueeze(2).to_broadcast([P, E, T])

            def v16(i):
                return rv[:, i, 0:16]

            iota_e = const("iota_e").unsqueeze(1).to_broadcast([P, T, E])
            link(dve.tensor_reduce(v16(0), logits[:, :, :], AX_X, ALU.max))
            dve.tensor_tensor(te(0), logits[:, :, :], over_e(v16(0)), ALU.subtract).then_inc(exp_in, 1)
            dve.wait_ge(bias_in, 64)
            link(dve.tensor_copy(b_hi[:, :], b_raw[:, :]))
            for base in (0, 64):
                dve.tensor_copy(bias_sb[base:base + 32, :], b_hi[base:base + 32, :].bitcast(F32))
                ins = dve.tensor_tensor(bias_sb[base + 32:base + 64, :], b_raw[base + 32:base + 64, :],
                                        b_hi[base + 32:base + 64, :].bitcast(F32), ALU.subtract)
            ins.then_inc(bias_ok, 1)
            dve.wait_ge(exp_ok, 1)
            link(dve.tensor_reduce(v16(1), te(1), AX_X, ALU.add))
            link(dve.reciprocal(v16(2), v16(1)))
            link(dve.tensor_tensor(te(2), te(1), over_e(v16(2)), ALU.mult))
            def pick(p, cand, mask, top, low):
                link(dve.tensor_reduce(v16(top), te(p), AX_X, ALU.max))
                link(dve.tensor_tensor(te(cand), te(p), over_e(v16(top)), ALU.is_equal))
                link(dve.scalar_tensor_tensor(te(cand), te(cand), -64.0, iota_e, ALU.mult, ALU.add))
                link(dve.tensor_reduce(v16(low), te(cand), AX_X, ALU.min))
                link(dve.tensor_tensor(te(mask), te(cand), over_e(v16(low)), ALU.is_equal))

            pick(2, 3, 4, 3, 4)
            link(dve.scalar_tensor_tensor(te(5), te(4), -4.0, te(2), ALU.mult, ALU.add))
            pick(5, 3, 6, 5, 6)
            dve.tensor_tensor(et(7).rearrange("p e t -> p t e"), te(4), te(6), ALU.add).then_inc(picked, 1)
            link(dve.tensor_tensor(v16(10), v16(3), v16(5), ALU.add))
            link(dve.tensor_scalar(v16(10), v16(10), 1e-9, None, ALU.max))
            link(dve.reciprocal(v16(11), v16(10)))
            dve.tensor_tensor(rv[:, 7, 0:T], v16(3), v16(11), ALU.mult)
            link(dve.tensor_tensor(rv[:, 7, T:2 * T], v16(5), v16(11), ALU.mult))
            split(0, 0, 1)
            split(0, 1, 2)
            split(1, 0, 1)
            dve.wait_ge(ranks, 1)
            within = ps[:, 0, 0:E * T]
            totals = ps[:, 1, 0:E * T]
            link(dve.tensor_tensor_scan(rt[:, 8, :], const("scan_keep"), totals, 0.0, ALU.mult, ALU.add))
            link(dve.tensor_tensor(rt[:, 9, :], rt[:, 8, :], totals, ALU.subtract))
            link(dve.tensor_tensor(rt[:, 9, :], rt[:, 9, :], within, ALU.add))
            link(dve.tensor_tensor(te(10), et(8)[:, :, T - 1:T].to_broadcast([P, E, E]),
                                   const("full_tiles").unsqueeze(1).to_broadcast([P, E, E]), ALU.is_gt))
            link(dve.tensor_reduce(v16(12), te(10), AX_X, ALU.add))
            link(dve.tensor_scalar(v16(12), v16(12), 1.0, None, ALU.max))
            link(dve.tensor_tensor_scan(v16(13), const("ones")[:, 0:E], v16(12), 0.0, ALU.mult, ALU.add))
            link(dve.tensor_tensor(v16(13), v16(13), v16(12), ALU.subtract))
            link(dve.tensor_scalar(v16(14), v16(13), float(P), None, ALU.mult))
            link(dve.tensor_tensor(et(9), et(9), over_t(v16(14)), ALU.add))
            for k, mask in ((0, 4), (1, 6)):
                link(dve.tensor_tensor(te(11), te(mask), et(9).rearrange("p e t -> p t e"), ALU.mult))
                link(dve.tensor_reduce(rv[:, 15, k * T:(k + 1) * T], te(11), AX_X, ALU.add))
            pos = rv[:, 15, :]
            pos_i = rt[:, 12, 0:32].bitcast(I32)
            hi_i = rt[:, 12, 32:64].bitcast(I32)
            lo_i = rt[:, 12, 64:96].bitcast(I32)
            pos_slot = rt[:, 12, 96:128]
            pos_row = rt[:, 12, 128:160]
            link(dve.tensor_copy(pos_i, pos))
            link(dve.tensor_scalar(hi_i, pos_i, 7, None, ALU.arith_shift_right))
            link(dve.tensor_scalar(lo_i, pos_i, P - 1, None, ALU.bitwise_and))
            link(dve.tensor_copy(pos_slot, hi_i))
            link(dve.tensor_copy(pos_row, lo_i))
            link(dve.tensor_copy(rt[:, 13, 0:32].bitcast(F32R), rv[:, 7, :]))
            link(dve.tensor_tensor(rt[:, 13, 32:64], rv[:, 7, :], rt[:, 13, 0:32], ALU.subtract))
            for i in range(2):
                dve.wait_ge(mid_out[i], 16 * T)
            dve.wait_ge(router_mm, T)
            A = TOP * T
            link(dve.tensor_tensor(hit_row[:, :, :], const("iota_row").unsqueeze(1).to_broadcast([P, A, P]),
                                   pos_row.unsqueeze(2).to_broadcast([P, A, P]), ALU.is_equal))
            link(dve.tensor_tensor(hit_slot[:, :].rearrange("p (a s) -> p a s", a=A),
                                   const("iota_slot").unsqueeze(1).to_broadcast([P, A, TAB]),
                                   pos_slot.unsqueeze(2).to_broadcast([P, A, TAB]), ALU.is_equal))
            for k in range(TOP):
                half = hit_slot[:, k * T * TAB:(k + 1) * T * TAB]
                vals = [const("token"), const("ones")[:, 0:T], rt[:, 13, k * T:(k + 1) * T],
                        rt[:, 13, 32 + k * T:32 + (k + 1) * T]]
                if k:
                    dve.wait_ge(table_mm, 1)
                for n, v in enumerate(vals):
                    ins = dve.tensor_tensor(hit_val[:, n, :].rearrange("p (a s) -> p a s", a=T),
                                            half.rearrange("p (a s) -> p a s", a=T),
                                            v.unsqueeze(2).to_broadcast([P, T, TAB]), ALU.mult)
                ins.then_inc(hits_ok, 1)
            slot_f = rt[:, 11, 0:TAB]
            started = rt[:, 0:4, :].rearrange("p a b -> p (a b)")[:, 0:TAB * E].rearrange("p (s e) -> p s e", e=E)
            link(dve.tensor_tensor(started, const("iota_slot").unsqueeze(2).to_broadcast([P, TAB, E]),
                                   v16(13).unsqueeze(1).to_broadcast([P, TAB, E]), ALU.is_ge))
            link(dve.tensor_reduce(slot_f, started, AX_X, ALU.add))
            link(dve.tensor_scalar(slot_f, slot_f, -1.0, None, ALU.add))
            link(dve.tensor_copy(slot_e[:, :], slot_f))
            link(dve.tensor_scalar(sel1_col[:, :], slot_f, const("is_bias1"), None, ALU.is_equal))
            link(dve.tensor_scalar(sel2_col[:, :], slot_f, const("is_bias2"), None, ALU.is_equal))
            new = rt[:, 11, 64:64 + TAB]
            not_last = rt[:, 11, 128:128 + TAB]
            link(dve.tensor_scalar(not_last, slot_f, float(E - 1), None, ALU.is_lt))
            link(dve.memset(new, 0.0))
            link(dve.tensor_tensor(new[:, 0:TAB - 1], slot_f[:, 1:TAB], slot_f[:, 0:TAB - 1], ALU.not_equal))
            link(dve.tensor_tensor(new[:, 0:TAB - 1], new[:, 0:TAB - 1], not_last[:, 1:TAB], ALU.mult))
            link(dve.tensor_copy(prep1[:, :], new))
            link(dve.memset(prep2[:, 0:1], 1))
            link(dve.tensor_copy(prep2[:, 1:TAB], new[:, 0:TAB - 1]))
            dve.wait_ge(table_mm, 2)
            tab = ps[:, 2, 0:4 * TAB].rearrange("p (n s) -> p n s", n=4)
            link(dve.tensor_copy(tok_i[:, :], tab[:, 0, :]))
            link(dve.tensor_scalar(rt[:, 10, 0:TAB], tab[:, 1, :], -1.0, 1.0, ALU.mult, ALU.add))
            link(dve.scalar_tensor_tensor(rt[:, 10, 64:64 + TAB], rt[:, 10, 0:TAB], const("dump_row"), tab[:, 0, :],
                                          ALU.mult, ALU.add))
            link(dve.tensor_copy(scat_i[:, :], rt[:, 10, 64:64 + TAB]))
            link(dve.tensor_copy(rt[:, 10, 128:128 + TAB], tab[:, 2, :]))
            dve.tensor_tensor(gate[:, :], rt[:, 10, 128:128 + TAB], tab[:, 3, :], ALU.add).then_inc(table_ok, 1)

            def slot_x_lo(s, par):
                dve.wait_ge(x_hi_ok, s + 1)
                dve.tensor_tensor(xt_lo[:, par, :], xt_ps(par), xt_hi[:, par, :].bitcast(F32), ALU.subtract).then_inc(x_lo_ok, 1)

            def slot_stats(s, par):
                dve.wait_ge(mm1, s + 1)
                link(dve.bn_stats(h_stats[:, par, :], h_ps(par)))
                dve.sem_inc(dve_turn, 1)
                dve.bn_aggr(h_mv[:, par, :], h_stats[:, par, :]).then_inc(h_var, 1)

            slot_x_lo(0, 0)
            slot_x_lo(1, 1)
            slot_stats(0, 0)
            dve.sem_inc(y_ok, 1)
            with dve.Fori(0, SLOTS // 2) as j:
                own.enter(j, 2)
                for par in range(2):
                    s = j * 2 + par
                    e_s = dve.value_load(slot_e[0:1, bass.ds(s, 1)], min_val=0, max_val=E - 1)
                    e_n = dve.value_load(slot_e[0:1, bass.ds(s + 1, 1)], min_val=0, max_val=E - 1)
                    do1 = dve.value_load(prep1[0:1, bass.ds(s, 1)], min_val=0, max_val=1)
                    do2 = dve.value_load(prep2[0:1, bass.ds(s, 1)], min_val=0, max_val=1)
                    dve.wait_ge(g_hi_ok, s + 1)
                    dve.tensor_tensor(gt_lo[:, par, :], g_sb[:, par, :], gt_hi[:, par, :].bitcast(F32),
                                      ALU.subtract).then_inc(g_lo_ok, 1)
                    slot_x_lo(s + 2, par)
                    slot_stats(s + 1, 1 - par)
                    for n, do, e in ((0, do1, e_n), (1, do2, e_s)):
                        with dve.If(do == 1):
                            at = bass.ds(((e + 1) & 1) * (C * D), C * D)
                            dve.wait_ge(split_hi[n], e + 2)
                            dve.tensor_tensor(w_lo[:, n, at], w_raw[:, n, :, :].rearrange("p a n -> p (a n)")[:, at],
                                              w_hi[:, n, at].bitcast(F32), ALU.subtract).then_inc(split_lo[n], 1)
                    dve.wait_ge(mm2, s + 1)
                    dve.wait_ge(scattered, s * 16 + 16)
                    dve.tensor_scalar(y_sb[:, :], y_ps, gate[:, bass.ds(s, 1)], None, ALU.mult).then_inc(y_ok, 1)
                own.leave(SLOTS // 2)

        @block.tensor
        def _(pe):
            ident = const("ident")
            ones = const("ones")
            pe.wait_ge(consts_in, 96)
            for i, col in ((0, 8), (1, 15)):
                pe.wait_ge(w_means, i + 1)
                pe.matmul(side_bank(0, i)[:, 0:1], ones, small[:, col:col + 1], start=True, stop=True).then_inc(w_sums, 1)

            def transpose_x(t, par):
                pe.wait_ge(xq_ready, t + 1)
                for c in range(C):
                    ins = pe.transpose(side_bank(0, par)[:, c * P:(c + 1) * P], xq[:, par, c * P:(c + 1) * P], ident)
                ins.then_inc(xq_t, 1)

            def support(t, par):
                pe.wait_ge(xq_lo_ok, t + 1)
                for part in (xq_hi, xq_lo):
                    for c in range(C):
                        ins = pe.matmul(side_bank(0, 2 + par), part[:, par, c * P:(c + 1) * P],
                                        w_int[:, c * D:(c + 1) * D],
                                        start=part is xq_hi and c == 0, stop=part is xq_lo and c == C - 1)
                ins.then_inc(sup_mm, 1)

            sup_flat = sup[:, :, :].rearrange("p t d -> p (t d)")

            def step(q, m, par, n, first=False, last=False):
                pe.wait_ge(adj_lo_ok, n)
                for k in range(2):
                    for i in range(TQ):
                        for part in (adj_hi, adj_lo):
                            ins = pe.matmul(acc_bank(q, i), part[:, par, k, i * P:(i + 1) * P],
                                            sup_flat[:, bass.ds((m * 2 + k) * D, D)],
                                            start=first and k == 0 and part is adj_hi,
                                            stop=last and k == 1 and part is adj_lo)
                ins.then_inc(adj_mm, 1)

            pe.sem_inc(adj_mm, 1)
            pe.wait_ge(w_ready, 1)
            transpose_x(0, 0)
            transpose_x(1, 1)
            support(0, 0)
            transpose_x(2, 0)
            support(1, 1)
            pe.wait_ge(sup_ok, 2)
            step(0, 0, 0, 1, first=True)
            with pe.Fori(0, MID) as j:
                for half in range(2):
                    t = j * 4 + 2 * half
                    transpose_x(t + 3, 1)
                    support(t + 2, 0)
                    transpose_x(t + 4, 0)
                    support(t + 3, 1)
                    pe.wait_ge(sup_ok, t + 4)
                    step(0, j * 2 + (1 + half), 1 - half, j * 2 + (2 + half))
            transpose_x(T - 1, 1)
            support(T - 2, 0)
            support(T - 1, 1)
            pe.wait_ge(sup_ok, T)
            step(0, STEPS - 1, 1, STEPS, last=True)

            def finish_t(t):
                pe.wait_ge(xn_ok, t + 1)
                if t >= 2:
                    pe.wait_ge(xn_t_ok, t - 1)
                for c in range(C):
                    ins = pe.transpose(side_bank(t // TQ + 1, t % 2)[:, c * P:(c + 1) * P],
                                       xn[:, t % 2, c * P:(c + 1) * P], ident)
                ins.then_inc(xn_tp, 1)

            def router(t):
                pe.wait_ge(xn_t_ok, t + 1)
                if t >= 2:
                    pe.wait_ge(logits_ok, t - 1)
                for c in range(C):
                    ins = pe.matmul(side_bank(t // TQ + 1, 2 + t % 2)[:, 0:E], xn_t[:, t % 2, c * P:(c + 1) * P],
                                    wr_sb[:, c * E:(c + 1) * E], start=c == 0, stop=c == C - 1)
                ins.then_inc(router_mm, 1)

            for q in range(1, QUARTERS):
                t0 = TQ * (q - 1)
                if q > 1:
                    pe.wait_ge(logits_ok, t0)
                n = STEPS * q + 1
                step(q, 0, 0, n, first=True)
                for jj in range(MID):
                    if jj == 0:
                        pe.wait_ge(acc_read, t0 + TQ)
                    finish_t(t0 + jj)
                    step(q, 2 * jj + 1, 1, n + 2 * jj + 1)
                    router(t0 + jj)
                    step(q, 2 * jj + 2, 0, n + 2 * jj + 2)
                finish_t(t0 + MID)
                step(q, STEPS - 1, 1, STEPS * (q + 1), last=True)
                router(t0 + MID)
            pe.wait_ge(acc_read, T)
            for t in range(T - TQ, T):
                finish_t(t)
                router(t)

            pe.wait_ge(picked, 1)
            chosen = rt[:, 7, :]
            pe.matmul(ps[:, 0, 0:E * T], const("tri"), chosen, start=True, stop=True)
            pe.matmul(ps[:, 1, 0:E * T], ones, chosen, start=True, stop=True).then_inc(ranks, 1)
            for k in range(TOP):
                pe.wait_ge(hits_ok, k + 1)
                for t in range(T):
                    rhs = hit_val[:, :, t * TAB:(t + 1) * TAB]
                    ins = pe.matmul(ps[:, 2, 0:4 * TAB].rearrange("p (n s) -> p n s", n=4), hit_row[:, k * T + t, :], rhs,
                                    start=k == 0 and t == 0, stop=k == TOP - 1 and t == T - 1)
                ins.then_inc(table_mm, 1)

            def rows_t(s, par, landed):
                pe.wait_ge(gathered[par], landed)
                for c in range(C):
                    ins = pe.transpose(xt_ps(par)[:, c * P:(c + 1) * P], xg[:, par, c * P:(c + 1) * P], ident)
                ins.then_inc(x_tp, 1)

            def layer(dst, n, par, e, act_hi, act_lo, sel, done):
                pe.matmul(dst, sel[:, par, :], bias_sb[:, :], start=True, stop=False)
                for c in range(C):
                    at = bass.ds((e & 1) * (C * D) + c * D, D)
                    pe.matmul(dst, act_hi[:, par, c * P:(c + 1) * P], w_hi[:, n, at], start=False, stop=False)
                    pe.matmul(dst, act_lo[:, par, c * P:(c + 1) * P], w_hi[:, n, at], start=False, stop=False)
                    ins = pe.matmul(dst, act_hi[:, par, c * P:(c + 1) * P], w_lo[:, n, at], start=False, stop=c == C - 1)
                ins.then_inc(done, 1)

            pe.wait_ge(table_ok, 1)
            rows_t(0, 0, 16)
            rows_t(1, 1, 16)
            pe.wait_ge(x_lo_ok, 1)
            pe.wait_ge(split_lo[0], 1)
            pe.wait_ge(sel_ok, 3)
            pe.wait_ge(bias_ok, 1)
            layer(h_ps(0), 0, 0, 0, xt_hi, xt_lo, sel1, mm1)
            with pe.Fori(0, SLOTS // 2) as j:
                for par in range(2):
                    s = j * 2 + par
                    e_s = pe.value_load(slot_e[0:1, bass.ds(s, 1)], min_val=0, max_val=E - 1)
                    e_n = pe.value_load(slot_e[0:1, bass.ds(s + 1, 1)], min_val=0, max_val=E - 1)
                    pe.wait_ge(h_hat_ok, s + 1)
                    for c in range(C):
                        ins = pe.transpose(ht_ps(par)[:, c * P:(c + 1) * P], h_hat[:, par, c * P:(c + 1) * P], ident)
                    ins.then_inc(h_tp, 1)
                    rows_t(s + 2, par, j * 16 + 32)
                    pe.wait_ge(x_lo_ok, s + 2)
                    pe.wait_ge(split_lo[0], e_n + 1)
                    pe.wait_ge(sel_ok, s * 2 + 3)
                    layer(h_ps(1 - par), 0, 1 - par, e_n, xt_hi, xt_lo, sel1, mm1)
                    pe.wait_ge(g_lo_ok, s + 1)
                    pe.wait_ge(split_lo[1], e_s + 1)
                    pe.wait_ge(sel_ok, s * 2 + 3)
                    pe.wait_ge(y_ok, s + 1)
                    layer(y_ps, 1, par, e_s, gt_hi, gt_lo, sel2, mm2)


_OUT_ROWS = N + P


def kernel(x, adj, L0_gnn_adj_scaling_factor, L0_gnn_weight, L0_gnn_wgt_alpha, L0_gnn_act_alpha, L0_gnn_act_alpha2,
           L0_ffn_Wr, L0_ffn_br, L0_ffn_W1, L0_ffn_b1, L0_ffn_g1, L0_ffn_be1, L0_ffn_W2, L0_ffn_b2):
    import concourse.bacc as bacc
    from concourse.bass_utils import run_bass_kernel_spmd

    def chunked(w):
        w = np.asarray(w)
        w = w.reshape(-1, C, P, w.shape[-1]).transpose(0, 2, 1, 3)
        return np.ascontiguousarray(w.reshape(-1, C * w.shape[-1]))

    def rows(v):
        return np.ascontiguousarray(np.broadcast_to(v, (P, v.size)))

    scalars = np.stack([np.asarray(v).reshape(()) for v in
                        (L0_gnn_adj_scaling_factor, L0_gnn_wgt_alpha, L0_gnn_act_alpha, L0_gnn_act_alpha2)])
    by_hidden = [np.ascontiguousarray(np.asarray(v).reshape(E * C, P).T) for v in (L0_ffn_g1, L0_ffn_be1)]
    ins = {
        "x": np.asarray(x),
        "adj_t": np.ascontiguousarray(np.asarray(adj).T),
        "gnn_w": chunked(L0_gnn_weight),
        "scalars": rows(scalars),
        "wr": chunked(L0_ffn_Wr),
        "br": rows(np.asarray(L0_ffn_br)),
        "w1": chunked(L0_ffn_W1),
        "b1": np.asarray(L0_ffn_b1),
        "g1": by_hidden[0],
        "be1": by_hidden[1],
        "w2": chunked(L0_ffn_W2),
        "b2": np.asarray(L0_ffn_b2),
        "consts": constants(),
    }
    nc = bacc.Bacc("TRN2", target_bir_lowering=False, num_devices=1)
    aps = {n: nc.dram_tensor(f"in_{n}", a.shape, mybir.dt.from_np(a.dtype), kind="ExternalInput").ap()
           for n, a in ins.items()}
    xn_rows = nc.dram_tensor("xn_rows", [N, D], F32, kind="Internal").ap()
    out = nc.dram_tensor("out", [_OUT_ROWS, D], F32, kind="ExternalOutput").ap()
    gnn_moe_program(nc, xn_rows=xn_rows, out=out, **aps)
    r = run_bass_kernel_spmd(nc, [{f"in_{n}": a for n, a in ins.items()}], core_ids=[0])
    return r.results[0]["out"][:N]
```

```python
from contextlib import ExitStack

import numpy as np

import concourse.bass as bass
from concourse import mybir

ALU = mybir.AluOpType
ACT = mybir.ActivationFunctionType
F32 = mybir.dt.float32
F32R = mybir.dt.float32r
I32 = mybir.dt.int32
AX_X = mybir.AxisListType.X

P = 128
N = 2048
D = 512
E = 16
T = N // P
C = D // P
TOP = 2
SLOTS = (TOP * N - E) // P + E
SLOTS += SLOTS % 2
TAB = SLOTS + 6
QUARTERS = 4
TQ = T // QUARTERS
STEPS = T // 2
LN_EPS = 1e-5
MAGIC = 1.5 * 2.0 ** 23
N_ACT = 15.0
N_WGT = 7.0

_WIDTHS = [("ident", P), ("tri", P), ("ones", P), ("iota_row", P), ("iota_slot", TAB), ("iota_e", E),
           ("full_tiles", E), ("token_1", T), ("is_bias1", 1), ("is_bias2", 1), ("dump_row_1", 1),
           ("scan_keep", E * T), ("neg_half", 1), ("minus_one", 1)]
COLS, _at = {}, 0
for _name, _w in _WIDTHS:
    COLS[_name] = (_at, _at + _w)
    _at += _w
CONSTS = _at


def constants():
    k = np.zeros((P, CONSTS), np.float32)
    p = np.arange(P)

    def put(name, v):
        a, b = COLS[name]
        k[:, a:b] = v

    put("ident", np.eye(P))
    put("tri", p[:, None] < p[None, :])
    put("ones", 1.0)
    put("iota_row", p[None, :])
    put("iota_slot", np.arange(TAB)[None, :])
    put("iota_e", np.arange(E)[None, :])
    put("full_tiles", P * np.arange(E)[None, :])
    put("token_1", P * np.arange(T)[None, :] + p[:, None] + 1)
    put("is_bias1", np.where(p < 64, p % 32, 1000)[:, None])
    put("is_bias2", np.where(p >= 64, p % 32, 1000)[:, None])
    put("dump_row_1", (N + p + 1)[:, None])
    put("scan_keep", np.tile((np.arange(T) > 0).astype(np.float32), E)[None, :])
    put("neg_half", -0.5)
    put("minus_one", -1.0)
    return k


class Chain:

    def __init__(self, eng, sem):
        self.eng, self.sem = eng, sem
        self.base, self.n, self.i, self.per = 0, 0, None, 0

    def link(self, ins):
        self.n += 1
        ins.then_inc(self.sem, 1)
        at = self.base + self.n
        self.eng.wait_ge(self.sem, at if self.i is None else self.i * self.per + at)

    def enter(self, i, per):
        self.base, self.n, self.i, self.per = self.base + self.n, 0, i, per

    def leave(self, trips):
        assert self.n == self.per, (self.n, self.per)
        self.base, self.n, self.i = self.base + trips * self.per, 0, None


def gnn_moe_program(nc, x, adj_t, gnn_w, scalars, wr, br, w1, b1, g1, be1, w2, b2, consts, xn_rows, out):
    with ExitStack() as ctx:
        usable = nc.sbuf_usable_end
        first = (nc.sbuf_base + 31) // 32 * 32
        where = [first]

        def place(name, shape, dt):
            size = int(np.prod(shape[1:])) * 4
            t = nc.alloc_sbuf_tensor_at(name, shape, dt, offset=where[0])
            where[0] += (size + 31) // 32 * 32
            assert where[0] <= usable, (name, where[0], usable)
            return t

        def sem(name):
            return ctx.enter_context(nc.semaphore(name))

        k_sb = place("k_sb", [P, CONSTS], F32)
        sc = place("sc", [P, 4], F32)
        g1_sb = place("g1_sb", [P, E * C], F32)
        be1_sb = place("be1_sb", [P, E * C], F32)
        br_sb = place("br_sb", [P, E], F32)
        wr_sb = place("wr_sb", [P, C * E], F32)
        bias_sb = place("bias_sb", [P, D], F32R)
        w_raw = place("w_raw", [P, 2, 2, C * D], F32)
        logits = place("logits", [P, T, E], F32)
        small = place("small", [P, 64], F32)
        stats = place("stats", [P, 4, 6], F32)
        mv = place("mv", [P, T, 2], F32)
        rstd = place("rstd", [P, T, 2], F32)
        tok_i = place("tok_i", [P, TAB], I32)
        scat_i = place("scat_i", [P, TAB], I32)
        gate = place("gate", [P, TAB], F32)
        sel1_col = place("sel1_col", [P, TAB], F32)
        sel2_col = place("sel2_col", [P, TAB], F32)
        slot_e = place("slot_e", [P, TAB], I32)
        starts = place("starts", [P, TAB], I32)
        pairs = place("pairs", [P, 1], I32)
        end_fixed = where[0]

        sup = place("sup", [P, T, D], F32R)
        adj_raw = place("adj_raw", [P, 2, 2, D], F32)
        adj_hi = place("adj_hi", [P, 2, 2, D], F32R)
        adj_lo = place("adj_lo", [P, 2, 2, D], F32R)
        xq = place("xq", [P, 2, D], F32)
        xq_hi = place("xq_hi", [P, 2, D], F32R)
        xq_lo = place("xq_lo", [P, 2, D], F32R)
        end_adj = where[0]
        w_int = place("w_int", [P, C * D], F32R)
        x_sb = place("x_sb", [P, T, D], F32)
        xn = place("xn", [P, 2, D], F32)
        xn_t = place("xn_t", [P, 2, D], F32)
        gw_raw = place("gw_raw", [P, C * D], F32)
        relu_sb = place("relu_sb", [P, 2, D], F32)
        rt = place("rt", [P, 14, E * T], F32)
        rv = place("rv", [P, 16, 32], F32)
        b_raw = place("b_raw", [P, D], F32)
        b_hi = place("b_hi", [P, D], F32R)
        end_gnn = where[0]

        where[0] = end_fixed
        w_hi = place("w_hi", [P, 2, 2 * C * D], F32R)
        w_lo = place("w_lo", [P, 2, 2 * C * D], F32R)
        end_w = where[0]
        where[0] = max(end_w, end_adj)
        ffn0 = where[0]
        xg = place("xg", [P, 2, D], F32)
        xt_hi = place("xt_hi", [P, 2, D], F32R)
        xt_lo = place("xt_lo", [P, 2, D], F32R)
        h_hat = place("h_hat", [P, 2, D], F32)
        g_sb = place("g_sb", [P, 2, D], F32)
        gt_hi = place("gt_hi", [P, 2, D], F32R)
        gt_lo = place("gt_lo", [P, 2, D], F32R)
        y_sb = place("y_sb", [P, 2, D], F32)
        sel1 = place("sel1", [P, 2, P], F32R)
        sel2 = place("sel2", [P, 2, P], F32R)
        idx_g = place("idx_g", [P, 2], I32)
        idx_s = place("idx_s", [P, 2], I32)
        h_stats = place("h_stats", [P, 2, 6], F32)
        h_mv = place("h_mv", [P, 2, 2], F32)
        h_rs = place("h_rs", [P, 2, 4], F32)
        hit_row_at = where[0]
        hit_row = place("hit_row", [P, TOP * T, P], F32R)
        assert where[0] <= end_gnn
        where[0] = ffn0
        hit_slot = place("hit_slot", [P, TOP * T * TAB], F32)
        hit_val = place("hit_val", [P, TOP, 3, T * TAB], F32R)
        assert where[0] <= hit_row_at

        ps = ctx.enter_context(nc.psum_tensor("ps", [P, 8, D], F32))

        def const(name):
            a, b = COLS[name]
            return k_sb[:, a:b]

        pos_row = rt[:, 12, 128:160]

        consts_in = sem("consts_in")
        scalars_in = sem("scalars_in")
        small_in = sem("small_in")
        gw_in = sem("gw_in")
        x_in = [sem(f"x_in{i}") for i in range(4)]
        adj_in = [sem(f"adj_in{i}") for i in range(2)]
        dve_own = sem("dve_own")
        pool_own = sem("pool_own")
        pool_turn = sem("pool_turn")
        dve_turn = sem("dve_turn")
        w_means = sem("w_means")
        w_sums = sem("w_sums")
        w_var = sem("w_var")
        w_rstd = sem("w_rstd")
        w_ready = sem("w_ready")
        x_var = sem("x_var")
        x_rstd = sem("x_rstd")
        xq_ready = sem("xq_ready")
        xq_t = sem("xq_t")
        xq_hi_ok = sem("xq_hi_ok")
        xq_lo_ok = sem("xq_lo_ok")
        sup_mm = sem("sup_mm")
        relu_ok = sem("relu_ok")
        sup_ok = sem("sup_ok")
        adj_hi_ok = sem("adj_hi_ok")
        adj_lo_ok = sem("adj_lo_ok")
        adj_mm = sem("adj_mm")
        acc_read = sem("acc_read")
        mid_ok = sem("mid_ok")
        mid_rstd = sem("mid_rstd")
        xn_ok = sem("xn_ok")
        xn_tp = sem("xn_tp")
        xn_t_ok = sem("xn_t_ok")
        router_mm = sem("router_mm")
        logits_ok = sem("logits_ok")
        mid_out = [sem(f"mid_out{i}") for i in range(2)]
        bias_in = sem("bias_in")
        bias_ok = sem("bias_ok")
        exp_in = sem("exp_in")
        exp_ok = sem("exp_ok")
        picked = sem("picked")
        ranks = sem("ranks")
        tok_ok = sem("tok_ok")
        hits_ok = sem("hits_ok")
        table_mm = sem("table_mm")
        table_ok = sem("table_ok")
        raw_in = [sem(f"raw{n}_in") for n in (1, 2)]
        split_hi = [sem(f"split{n}_hi") for n in (1, 2)]
        split_lo = [sem(f"split{n}_lo") for n in (1, 2)]
        gathered = [sem(f"gathered{i}") for i in range(2)]
        x_tp = sem("x_tp")
        x_hi_ok = sem("x_hi_ok")
        x_lo_ok = sem("x_lo_ok")
        sel_ok = sem("sel_ok")
        mm1 = sem("mm1")
        h_var = sem("h_var")
        h_rstd = sem("h_rstd")
        h_hat_ok = sem("h_hat_ok")
        h_tp = sem("h_tp")
        gelu_ok = sem("gelu_ok")
        g_hi_ok = sem("g_hi_ok")
        g_lo_ok = sem("g_lo_ok")
        mm2 = sem("mm2")
        y_ok = sem("y_ok")
        scattered = sem("scattered")

        block = ctx.enter_context(nc.Block())

        def acc_bank(q, i):
            return ps[:, 4 * (q % 2) + i, :]

        def side_bank(q, i):
            return ps[:, 4 * (1 - q % 2) + i, :]

        def xt_ps(par):
            return ps[:, par, :]

        def h_ps(par):
            return ps[:, 2 + par, :]

        def ht_ps(par):
            return ps[:, 4 + par, :]

        def y_ps(par):
            return ps[:, 6 + par, :]

        MID = 3

        @block.sync
        def _(sp):
            sp.dma_start(sc[:, :], scalars).then_inc(scalars_in, 16)
            sp.dma_start(gw_raw[:, :], gnn_w).then_inc(gw_in, 16)
            sp.dma_start(k_sb[:, :], consts).then_inc(consts_in, 16)
            for i in range(4):
                sp.dma_start(x_sb[:, 4 * i:4 * i + 4, :],
                             x[4 * i * P:(4 * i + 4) * P, :].rearrange("(t p) d -> p t d", p=P)).then_inc(x_in[i], 16)
            view = adj_t.rearrange("(s k p) n -> p s k n", p=P, k=2)

            def load_adj(q, m, par):
                return sp.dma_start(adj_raw[:, par, :, :],
                                    view[:, m:m + 1, :, q * D:(q + 1) * D].rearrange("p s k n -> p (s k) n")
                                    if isinstance(m, int) else
                                    view[:, bass.ds(m, 1), :, q * D:(q + 1) * D].rearrange("p s k n -> p (s k) n")
                                    ).then_inc(adj_in[par], 16)

            for q in range(QUARTERS):
                for par in range(2):
                    if q:
                        sp.wait_ge(adj_lo_ok, STEPS * q - 1 + par)
                    load_adj(q, par, par)
                with sp.Fori(1, STEPS // 2) as j:
                    for par in range(2):
                        sp.wait_ge(adj_lo_ok, j * 2 + (STEPS * q - 1 + par))
                        load_adj(q, j * 2 + par, par)
            w_dram = (w1, w2)
            HALF = C * D // 2
            for e in range(2):
                for h in range(2):
                    for n in range(2):
                        if e or h:
                            sp.wait_ge(raw_in[n], 32 * e + 16 * h)
                        sp.dma_start(w_raw[:, n, e, h * HALF:(h + 1) * HALF],
                                     w_dram[n][e * P:(e + 1) * P, h * HALF:(h + 1) * HALF]).then_inc(raw_in[n], 16)
            with sp.Fori(1, E // 2) as j:
                for par in range(2):
                    for h in range(2):
                        for n in range(2):
                            sp.wait_ge(raw_in[n], j * 64 + (32 * par + 16 * h))
                            if h == 0:
                                sp.wait_ge(split_lo[n], j * 2 + (par - 1))
                            sp.dma_start(w_raw[:, n, par, h * HALF:(h + 1) * HALF],
                                         w_dram[n][bass.ds(j * 2 * P + par * P, P), h * HALF:(h + 1) * HALF]
                                         ).then_inc(raw_in[n], 16)

        @block.gpsimd
        def _(pool):
            own = Chain(pool, pool_own)
            pool.dma_start(g1_sb[:, :], g1).then_inc(small_in, 16)
            pool.dma_start(be1_sb[:, :], be1).then_inc(small_in, 16)
            pool.dma_start(br_sb[:, :], br).then_inc(small_in, 16)
            pool.dma_start(wr_sb[:, :], wr).then_inc(small_in, 16)
            neg_half = const("neg_half")
            own.link(pool.memset(b_raw[:, :], 0.0))
            for base, b in ((0, b1), (32, b1), (64, b2), (96, b2)):
                pool.dma_start(b_raw[base:base + E, :], b).then_inc(bias_in, 16)
            neg_half = const("neg_half")
            pool.wait_ge(consts_in, 16)
            for h in range(2):
                pool.dma_start(out[N + h * P // 2:N + (h + 1) * P // 2, :], k_sb[h * P // 2:(h + 1) * P // 2, 0:D]
                               ).then_inc(scattered, 16)
            pool.wait_ge(w_var, 1)
            pool.tensor_tensor(small[:, 13:14], small[:, 12:13], neg_half, ALU.pow).then_inc(w_rstd, 1)
            pool.wait_ge(x_var, 1)
            pool.tensor_tensor(rstd[:, :, 0], rstd[:, :, 1], neg_half.to_broadcast([P, T]), ALU.pow).then_inc(x_rstd, 1)

            for t in range(T):
                pool.wait_ge(mid_ok, t + 1)
                own.link(pool.tensor_scalar(rstd[:, t, 1:2], mv[:, t, 1:2], LN_EPS, None, ALU.add))
                own.link(pool.tensor_tensor(rstd[:, t, 0:1], rstd[:, t, 1:2], neg_half, ALU.pow))
                own.link(pool.tensor_tensor(rstd[:, t, 1:2], mv[:, t, 0:1], rstd[:, t, 0:1], ALU.mult))
                pool.tensor_scalar(rstd[:, t, 1:2], rstd[:, t, 1:2], -1.0, None, ALU.mult).then_inc(mid_rstd, 1)

            def select(dst, par, col, s):
                return pool.tensor_copy(dst[:, par, :], col[:, bass.ds(s, 1)].to_broadcast([P, P]))

            def gather(par):
                return pool.indirect_dma_start(
                    xg[:, par, :], None, xn_rows,
                    bass.IndirectOffsetOnAxis(ap=idx_g[:, par:par + 1], axis=0)).then_inc(gathered[par], 16)

            def slot_rstd(par):
                own.link(pool.tensor_scalar(h_rs[:, par, 2:3], h_mv[:, par, 1:2], LN_EPS, None, ALU.add))
                own.link(pool.tensor_tensor(h_rs[:, par, 0:1], h_rs[:, par, 2:3], neg_half, ALU.pow))
                own.link(pool.tensor_tensor(h_rs[:, par, 3:4], h_mv[:, par, 0:1], h_rs[:, par, 0:1], ALU.mult))
                pool.tensor_tensor(h_rs[:, par, 1:2], h_rs[:, par, 3:4], const("minus_one"), ALU.mult).then_inc(h_rstd, 1)

            for i in range(2):
                pool.wait_ge(mid_out[i], 16 * T)
            pool.wait_ge(tok_ok, 1)
            for s in range(2):
                own.link(pool.tensor_copy(idx_g[:, s:s + 1], tok_i[:, s:s + 1]))
                gather(s)
            pool.wait_ge(table_ok, 1)
            pool.wait_ge(scattered, 32)
            select(sel1, 0, sel1_col, 0).then_inc(sel_ok, 1)
            select(sel1, 1, sel1_col, 1).then_inc(sel_ok, 1)
            select(sel2, 0, sel2_col, 0).then_inc(sel_ok, 1)
            for s in range(2, 5):
                pool.wait_ge(x_tp, s - 1)
                own.link(pool.tensor_copy(idx_g[:, s % 2:s % 2 + 1], tok_i[:, s:s + 1]))
                gather(s % 2)
                if s == 4:
                    select(sel1, 0, sel1_col, 2).then_inc(sel_ok, 1)
                if s >= 3:
                    pool.wait_ge(h_var, s - 2)
                    slot_rstd(s - 3)
            live = pool.value_load(pairs[0:1, 0:1], min_val=1, max_val=SLOTS // 2)
            with pool.Fori(0, SLOTS // 2) as j:
                with pool.If(j < live):
                    own.enter(j, 2 * 5)
                    for par in range(2):
                        s = j * 2 + par
                        pool.wait_ge(x_tp, s + 4)
                        pool.sem_inc(pool_turn, 1)
                        own.link(pool.tensor_copy(idx_g[:, 1 - par:2 - par], tok_i[:, bass.ds(s + 5, 1)]))
                        pool.sem_inc(pool_turn, 1)
                        gather(1 - par)
                        select(sel1, 1 - par, sel1_col, s + 3).then_inc(sel_ok, 1)
                        select(sel2, 1 - par, sel2_col, s + 1).then_inc(sel_ok, 1)
                        pool.wait_ge(h_var, s + 3)
                        pool.sem_inc(pool_turn, 1)
                        slot_rstd(par)
                        own.link(pool.tensor_copy(idx_s[:, par:par + 1], scat_i[:, bass.ds(s, 1)]))
                        pool.wait_ge(y_ok, s + 3)
                        pool.wait_ge(scattered, s * 16 + 32)
                        pool.sem_inc(pool_turn, 1)
                        pool.indirect_dma_start(
                            out, bass.IndirectOffsetOnAxis(ap=idx_s[:, par:par + 1], axis=0),
                            y_sb[:, par, :], None, compute_op=ALU.add).then_inc(scattered, 16)
                    own.leave(0)
            pool.wait_ge(scattered, live * 32 + 32)
            for par in range(2):
                pool.wait_ge(gathered[par], live * 16 + 16 * (3 - par))

        @block.scalar
        def _(act):
            def hi_step(par, arrived, before):
                act.wait_ge(adj_in[par], arrived)
                if before is not None:
                    act.wait_ge(adj_mm, before + 1)
                act.activation(adj_hi[:, par, :, :], adj_raw[:, par, :, :], ACT.Copy, scale=small[:, 0:1]).then_inc(adj_hi_ok, 1)

            def g_hi(t, par):
                act.wait_ge(xq_t, t + 1)
                act.activation(xq_hi[:, par, :], side_bank(0, par), ACT.Copy, bias=-MAGIC).then_inc(xq_hi_ok, 1)

            def g_relu(t, par):
                act.wait_ge(sup_mm, t + 1)
                act.activation(relu_sb[:, par, :], side_bank(0, 2 + par), ACT.Relu, scale=small[:, 5:6]).then_inc(relu_ok, 1)

            def finish_xn(t):
                act.wait_ge(mid_rstd, t + 1)
                if t >= 2:
                    act.wait_ge(xn_tp, t - 1)
                    act.wait_ge(mid_out[t % 2], 32 * (t // 2))
                act.activation(xn[:, t % 2, :], x_sb[:, t, :], ACT.Identity, scale=rstd[:, t, 0:1],
                               bias=rstd[:, t, 1:2]).then_inc(xn_ok, 1)
                act.dma_start(out[t * P:(t + 1) * P, :], x_sb[:, t, :]).then_inc(mid_out[t % 2], 16)
                act.wait_ge(xn_ok, t + 1)
                act.dma_start(xn_rows[t * P:(t + 1) * P, :], xn[:, t % 2, :]).then_inc(mid_out[t % 2], 16)

            def finish_t(t):
                act.wait_ge(xn_tp, t + 1)
                act.activation(xn_t[:, t % 2, :], side_bank(t // TQ + 1, t % 2), ACT.Copy).then_inc(xn_t_ok, 1)

            act.wait_ge(w_ready, 1)
            g_hi(0, 0)
            g_hi(1, 1)
            g_relu(0, 0)
            hi_step(0, 16, None)
            g_hi(2, 0)
            g_relu(1, 1)
            with act.Fori(0, MID) as j:
                for half in range(2):
                    par = 1 - half
                    g_hi(j * 4 + (2 * half + 3), 1)
                    g_relu(j * 4 + (2 * half + 2), 0)
                    hi_step(par, j * 16 + 16 * (1 + half), j * 2 + half)
                    g_hi(j * 4 + (2 * half + 4), 0)
                    g_relu(j * 4 + (2 * half + 3), 1)
            g_hi(T - 1, 1)
            g_relu(T - 2, 0)
            hi_step(1, 16 * (STEPS // 2), STEPS - 2)
            g_relu(T - 1, 1)
            for q in range(1, QUARTERS):
                t0 = TQ * (q - 1)
                in0 = 16 * (STEPS // 2) * q
                hi_step(0, in0 + 16, STEPS * q - 1)
                for jj in range(MID):
                    hi_step(1, in0 + 16 * (jj + 1), STEPS * q + 2 * jj)
                    finish_xn(t0 + jj)
                    hi_step(0, in0 + 16 * (jj + 2), STEPS * q + 2 * jj + 1)
                    finish_t(t0 + jj)
                hi_step(1, in0 + 16 * (STEPS // 2), STEPS * (q + 1) - 2)
                finish_xn(t0 + MID)
                finish_t(t0 + MID)
            def split(n, par, arrived):
                act.wait_ge(raw_in[n], arrived)
                act.activation(w_hi[:, n, par * C * D:(par + 1) * C * D], w_raw[:, n, par, :], ACT.Copy).then_inc(split_hi[n], 1)

            act.wait_ge(adj_mm, STEPS * QUARTERS + 1)
            act.wait_ge(small_in, 64)
            split(0, 0, 32)
            for t in range(T - TQ, T):
                finish_xn(t)
                if t > T - TQ:
                    finish_t(t - 1)
            finish_t(T - 1)
            split(0, 1, 64)
            split(1, 0, 32)
            act.wait_ge(exp_in, 1)
            act.activation(rt[:, 1, :], rt[:, 0, :], ACT.Exp).then_inc(exp_ok, 1)

            def slot_x_hi(s, par):
                act.wait_ge(x_tp, s + 1)
                act.activation(xt_hi[:, par, :], xt_ps(par), ACT.Copy).then_inc(x_hi_ok, 1)

            def slot_h_hat(s, par):
                act.wait_ge(h_rstd, s + 1)
                act.activation(h_hat[:, par, :], h_ps(par), ACT.Identity, scale=h_rs[:, par, 0:1],
                               bias=h_rs[:, par, 1:2]).then_inc(h_hat_ok, 1)

            def split_next(n, e, start):
                with act.If(start == 1):
                    at = bass.ds(((e + 1) & 1) * (C * D), C * D)
                    act.wait_ge(raw_in[n], e * 32 + 64)
                    act.activation(w_hi[:, n, at], w_raw[:, n, :, :].rearrange("p a n -> p (a n)")[:, at],
                                   ACT.Copy).then_inc(split_hi[n], 1)

            act.wait_ge(exp_ok, 1)
            act.preload_act_table(ACT.Gelu)
            act.wait_ge(table_ok, 1)
            e_1 = act.value_load(slot_e[0:1, 1:2], min_val=0, max_val=E - 1)
            start_1 = act.value_load(starts[0:1, 1:2], min_val=0, max_val=1)
            live = act.value_load(pairs[0:1, 0:1], min_val=1, max_val=SLOTS // 2)
            slot_x_hi(0, 0)
            slot_x_hi(1, 1)
            slot_h_hat(0, 0)
            slot_x_hi(2, 0)
            split_next(0, e_1, start_1)
            with act.Fori(0, SLOTS // 2) as j:
                with act.If(j < live):
                    for par in range(2):
                        s = j * 2 + par
                        e_s = act.value_load(slot_e[0:1, bass.ds(s, 1)], min_val=0, max_val=E - 1)
                        e_a = act.value_load(slot_e[0:1, bass.ds(s + 2, 1)], min_val=0, max_val=E - 1)
                        start_s = act.value_load(starts[0:1, bass.ds(s, 1)], min_val=0, max_val=1)
                        start_a = act.value_load(starts[0:1, bass.ds(s + 2, 1)], min_val=0, max_val=1)
                        act.wait_ge(h_tp, s + 1)
                        for c in range(C):
                            ins = act.activation(g_sb[:, par, c * P:(c + 1) * P], ht_ps(par)[:, c * P:(c + 1) * P],
                                                 ACT.Gelu, scale=g1_sb[:, bass.ds(e_s * C + c, 1)],
                                                 bias=be1_sb[:, bass.ds(e_s * C + c, 1)])
                        ins.then_inc(gelu_ok, 1)
                        act.wait_ge(gelu_ok, s + 1)
                        act.activation(gt_hi[:, par, :], g_sb[:, par, :], ACT.Copy).then_inc(g_hi_ok, 1)
                        slot_h_hat(s + 1, 1 - par)
                        slot_x_hi(s + 3, 1 - par)
                        split_next(0, e_a, start_a)
                        split_next(1, e_s, start_s)

        @block.vector
        def _(dve):
            own = Chain(dve, dve_own)
            link = own.link
            dve.wait_ge(scalars_in, 16)

            link(dve.reciprocal(small[:, 0:4], sc[:, 0:4]))
            link(dve.tensor_scalar(small[:, 4:5], sc[:, 0:1], sc[:, 3:4], 1.0 / N_ACT, ALU.mult, ALU.mult))
            link(dve.tensor_scalar(small[:, 6:7], sc[:, 2:3], 1.0 / N_ACT, None, ALU.mult))
            link(dve.tensor_scalar(small[:, 7:8], sc[:, 1:2], 1.0 / N_WGT, None, ALU.mult))
            link(dve.tensor_tensor(small[:, 5:6], small[:, 6:7], small[:, 7:8], ALU.mult))

            dve.wait_ge(gw_in, 16)
            for c in range(C):
                ins = dve.bn_stats(stats[:, c, :], gw_raw[:, c * D:(c + 1) * D])
            link(ins)
            dve.bn_aggr(small[:, 8:10], stats[:, :, :].rearrange("p a b -> p (a b)")).then_inc(w_means, 1)
            dve.wait_ge(w_sums, 1)
            link(dve.tensor_scalar(small[:, 10:11], side_bank(0, 0)[:, 0:1], 1.0 / P, None, ALU.mult))
            link(dve.tensor_tensor(small[:, 11:12], small[:, 8:9], small[:, 10:11], ALU.subtract))
            link(dve.tensor_tensor(small[:, 14:15], small[:, 11:12], small[:, 11:12], ALU.mult))
            dve.tensor_tensor(small[:, 15:16], small[:, 14:15], small[:, 9:10], ALU.add).then_inc(w_means, 1)
            dve.wait_ge(w_sums, 2)
            dve.tensor_scalar(small[:, 12:13], side_bank(0, 1)[:, 0:1], D * D / (D * D - 1.0) / P, None,
                              ALU.mult).then_inc(w_var, 1)
            for t in range(T):
                if t % 4 == 0:
                    dve.wait_ge(x_in[t // 4], 16)
                ins = dve.bn_stats(stats[:, t % 4, :], x_sb[:, t, :])
                if t % 4 == 3:
                    link(ins)
                    for u in range(4):
                        ins = dve.bn_aggr(mv[:, t - 3 + u, :], stats[:, u, :])
                    link(ins)
            dve.tensor_scalar(rstd[:, :, 1], mv[:, :, 1], LN_EPS, None, ALU.add).then_inc(x_var, 1)
            dve.wait_ge(w_rstd, 1)
            link(dve.tensor_scalar(gw_raw[:, :], gw_raw[:, :], small[:, 10:11], small[:, 13:14], ALU.subtract, ALU.mult))
            link(dve.tensor_scalar(gw_raw[:, :], gw_raw[:, :], small[:, 1:2], 1.0, ALU.mult, ALU.min))
            link(dve.tensor_scalar(gw_raw[:, :], gw_raw[:, :], -1.0, N_WGT, ALU.max, ALU.mult))
            dve.tensor_scalar(w_int[:, :], gw_raw[:, :], MAGIC, MAGIC, ALU.add, ALU.subtract).then_inc(w_ready, 1)
            dve.wait_ge(x_rstd, 1)

            def x_tile(t):
                return x_sb[:, :, :].rearrange("p t d -> p (t d)")[:, bass.ds(t * D, D)]

            def sup_tile(t):
                return sup[:, :, :].rearrange("p t d -> p (t d)")[:, bass.ds(t * D, D)]

            def mean_of(t):
                return mv[:, :, :].rearrange("p t d -> p (t d)")[:, bass.ds(t * 2, 1)]

            def rstd_of(t):
                return rstd[:, :, :].rearrange("p t d -> p (t d)")[:, bass.ds(t * 2, 1)]

            def quantise_x(t, par):
                link(dve.tensor_scalar(xq[:, par, :], x_tile(t), mean_of(t), rstd_of(t), ALU.subtract, ALU.mult))
                link(dve.tensor_scalar(xq[:, par, :], xq[:, par, :], small[:, 2:3], 1.0, ALU.mult, ALU.min))
                dve.tensor_scalar(xq[:, par, :], xq[:, par, :], N_ACT, MAGIC, ALU.mult, ALU.add).then_inc(xq_ready, 1)

            def x_lo(t, par):
                dve.wait_ge(xq_hi_ok, t + 1)
                dve.scalar_tensor_tensor(xq_lo[:, par, :], side_bank(0, par), MAGIC, xq_hi[:, par, :].bitcast(F32),
                                         ALU.subtract, ALU.subtract).then_inc(xq_lo_ok, 1)

            def quantise_sup(t, par):
                dve.wait_ge(relu_ok, t + 1)
                link(dve.tensor_scalar(relu_sb[:, par, :], relu_sb[:, par, :], small[:, 3:4], 1.0, ALU.mult, ALU.min))
                link(dve.tensor_scalar(relu_sb[:, par, :], relu_sb[:, par, :], N_ACT, MAGIC, ALU.mult, ALU.add))
                dve.tensor_scalar(sup_tile(t), relu_sb[:, par, :], MAGIC, None, ALU.subtract).then_inc(sup_ok, 1)

            def lo_step(par, n):
                dve.wait_ge(adj_hi_ok, n)
                dve.scalar_tensor_tensor(adj_lo[:, par, :, :].rearrange("p a b -> p (a b)"),
                                         adj_raw[:, par, :, :].rearrange("p a b -> p (a b)"), small[:, 0:1],
                                         adj_hi[:, par, :, :].rearrange("p a b -> p (a b)").bitcast(F32),
                                         ALU.mult, ALU.subtract).then_inc(adj_lo_ok, 1)

            quantise_x(0, 0)
            quantise_x(1, 1)
            x_lo(0, 0)
            quantise_x(2, 0)
            x_lo(1, 1)
            quantise_sup(0, 0)
            lo_step(0, 1)
            quantise_x(3, 1)
            x_lo(2, 0)
            quantise_sup(1, 1)
            with dve.Fori(0, MID) as j:
                own.enter(j, 4 * 4)
                for half in range(2):
                    t = j * 4 + 2 * half
                    quantise_x(t + 4, 0)
                    x_lo(t + 3, 1)
                    quantise_sup(t + 2, 0)
                    lo_step(1 - half, j * 2 + (2 + half))
                    quantise_x(t + 5, 1)
                    x_lo(t + 4, 0)
                    quantise_sup(t + 3, 1)
                own.leave(MID)
            x_lo(T - 1, 1)
            quantise_sup(T - 2, 0)
            lo_step(1, STEPS)
            quantise_sup(T - 1, 1)

            def split(n, par, ready):
                dve.wait_ge(split_hi[n], ready)
                dve.tensor_tensor(w_lo[:, n, par * C * D:(par + 1) * C * D], w_raw[:, n, par, :],
                                  w_hi[:, n, par * C * D:(par + 1) * C * D].bitcast(F32), ALU.subtract).then_inc(split_lo[n], 1)

            def add_gnn(t):
                dve.scalar_tensor_tensor(x_sb[:, t, :], acc_bank(t // TQ, t % TQ), small[:, 4:5], x_sb[:, t, :],
                                         ALU.mult, ALU.add).then_inc(acc_read, 1)

            def statistics(t):
                dve.wait_ge(acc_read, t + 1)
                link(dve.bn_stats(stats[:, t % 4, :], x_sb[:, t, :]))
                dve.bn_aggr(mv[:, t, :], stats[:, t % 4, :]).then_inc(mid_ok, 1)

            def add_br(t):
                dve.wait_ge(router_mm, t + 1)
                dve.tensor_tensor(logits[:, t, :], side_bank(t // TQ + 1, 2 + t % 2)[:, 0:E], br_sb[:, :],
                                  ALU.add).then_inc(logits_ok, 1)

            for q in range(1, QUARTERS):
                t0 = TQ * (q - 1)
                lo_step(0, STEPS * q + 1)
                dve.wait_ge(adj_mm, STEPS * q + 1)
                for t in range(t0, t0 + TQ):
                    add_gnn(t)
                statistics(t0)
                for jj in range(MID):
                    lo_step(1, STEPS * q + 2 * jj + 2)
                    lo_step(0, STEPS * q + 2 * jj + 3)
                    statistics(t0 + jj + 1)
                    add_br(t0 + jj)
                lo_step(1, STEPS * (q + 1))
                add_br(t0 + MID)
            dve.wait_ge(adj_mm, STEPS * QUARTERS + 1)
            for t in range(T - TQ, T):
                add_gnn(t)
            for t in range(T - TQ, T):
                statistics(t)
            split(0, 0, 1)
            for t in range(T - TQ, T):
                add_br(t)
            dve.wait_ge(small_in, 64)
            dve.wait_ge(logits_ok, T)

            def te(i):
                return rt[:, i, :].rearrange("p (t e) -> p t e", e=E)

            def et(i):
                return rt[:, i, :].rearrange("p (e t) -> p e t", t=T)

            def over_e(v):
                return v.unsqueeze(2).to_broadcast([P, T, E])

            def over_t(v):
                return v.unsqueeze(2).to_broadcast([P, E, T])

            def v16(i):
                return rv[:, i, 0:16]

            iota_e = const("iota_e").unsqueeze(1).to_broadcast([P, T, E])
            link(dve.tensor_reduce(v16(0), logits[:, :, :], AX_X, ALU.max))
            dve.tensor_tensor(te(0), logits[:, :, :], over_e(v16(0)), ALU.subtract).then_inc(exp_in, 1)
            dve.wait_ge(bias_in, 64)
            link(dve.tensor_copy(b_hi[:, :], b_raw[:, :]))
            for base in (0, 64):
                dve.tensor_copy(bias_sb[base:base + 32, :], b_hi[base:base + 32, :].bitcast(F32))
                ins = dve.tensor_tensor(bias_sb[base + 32:base + 64, :], b_raw[base + 32:base + 64, :],
                                        b_hi[base + 32:base + 64, :].bitcast(F32), ALU.subtract)
            ins.then_inc(bias_ok, 1)
            dve.wait_ge(exp_ok, 1)
            link(dve.tensor_reduce(v16(1), te(1), AX_X, ALU.add))
            link(dve.reciprocal(v16(2), v16(1)))
            link(dve.tensor_tensor(te(2), te(1), over_e(v16(2)), ALU.mult))
            def pick(p, cand, mask, top, low):
                link(dve.tensor_reduce(v16(top), te(p), AX_X, ALU.max))
                link(dve.tensor_tensor(te(cand), te(p), over_e(v16(top)), ALU.is_equal))
                link(dve.scalar_tensor_tensor(te(cand), te(cand), -64.0, iota_e, ALU.mult, ALU.add))
                link(dve.tensor_reduce(v16(low), te(cand), AX_X, ALU.min))
                link(dve.tensor_tensor(te(mask), te(cand), over_e(v16(low)), ALU.is_equal))

            pick(2, 3, 4, 3, 4)
            link(dve.scalar_tensor_tensor(te(5), te(4), -4.0, te(2), ALU.mult, ALU.add))
            pick(5, 3, 6, 5, 6)
            dve.tensor_tensor(et(7).rearrange("p e t -> p t e"), te(4), te(6), ALU.add).then_inc(picked, 1)
            link(dve.tensor_tensor(v16(10), v16(3), v16(5), ALU.add))
            link(dve.tensor_scalar(v16(10), v16(10), 1e-9, None, ALU.max))
            link(dve.reciprocal(v16(11), v16(10)))
            dve.tensor_tensor(rv[:, 7, 0:T], v16(3), v16(11), ALU.mult)
            link(dve.tensor_tensor(rv[:, 7, T:2 * T], v16(5), v16(11), ALU.mult))
            dve.wait_ge(ranks, 1)
            within = ps[:, 0, 0:E * T]
            totals = ps[:, 1, 0:E * T]
            link(dve.tensor_tensor_scan(rt[:, 8, :], const("scan_keep"), totals, 0.0, ALU.mult, ALU.add))
            link(dve.tensor_tensor(rt[:, 9, :], rt[:, 8, :], totals, ALU.subtract))
            link(dve.tensor_tensor(rt[:, 9, :], rt[:, 9, :], within, ALU.add))
            link(dve.tensor_tensor(te(10), et(8)[:, :, T - 1:T].to_broadcast([P, E, E]),
                                   const("full_tiles").unsqueeze(1).to_broadcast([P, E, E]), ALU.is_gt))
            link(dve.tensor_reduce(v16(12), te(10), AX_X, ALU.add))
            link(dve.tensor_scalar(v16(12), v16(12), 1.0, None, ALU.max))
            link(dve.tensor_tensor_scan(v16(13), const("ones")[:, 0:E], v16(12), 0.0, ALU.mult, ALU.add))
            link(dve.tensor_tensor(v16(13), v16(13), v16(12), ALU.subtract))
            link(dve.tensor_scalar(v16(14), v16(13), float(P), None, ALU.mult))
            link(dve.tensor_tensor(et(9), et(9), over_t(v16(14)), ALU.add))
            for k, mask in ((0, 4), (1, 6)):
                link(dve.tensor_tensor(te(11), te(mask), et(9).rearrange("p e t -> p t e"), ALU.mult))
                link(dve.tensor_reduce(rv[:, 15, k * T:(k + 1) * T], te(11), AX_X, ALU.add))
            pos = rv[:, 15, :]
            pos_i = rt[:, 12, 0:32].bitcast(I32)
            hi_i = rt[:, 12, 32:64].bitcast(I32)
            lo_i = rt[:, 12, 64:96].bitcast(I32)
            pos_slot = rt[:, 12, 96:128]
            link(dve.tensor_copy(pos_i, pos))
            link(dve.tensor_scalar(hi_i, pos_i, 7, None, ALU.arith_shift_right))
            link(dve.tensor_scalar(lo_i, pos_i, P - 1, None, ALU.bitwise_and))
            link(dve.tensor_copy(pos_slot, hi_i))
            link(dve.tensor_copy(pos_row, lo_i))
            link(dve.tensor_copy(rt[:, 13, 0:32].bitcast(F32R), rv[:, 7, :]))
            link(dve.tensor_tensor(rt[:, 13, 32:64], rv[:, 7, :], rt[:, 13, 0:32], ALU.subtract))
            for i in range(2):
                dve.wait_ge(mid_out[i], 16 * T)
            A = TOP * T
            link(dve.tensor_tensor(hit_slot[:, :].rearrange("p (a s) -> p a s", a=A),
                                   const("iota_slot").unsqueeze(1).to_broadcast([P, A, TAB]),
                                   pos_slot.unsqueeze(2).to_broadcast([P, A, TAB]), ALU.is_equal))
            for k in range(TOP):
                dve.tensor_tensor(hit_row[:, k * T:(k + 1) * T, :], const("iota_row").unsqueeze(1).to_broadcast([P, T, P]),
                                  pos_row[:, k * T:(k + 1) * T].unsqueeze(2).to_broadcast([P, T, P]), ALU.is_equal)
                half = hit_slot[:, k * T * TAB:(k + 1) * T * TAB]
                vals = [const("token_1"), rt[:, 13, k * T:(k + 1) * T], rt[:, 13, 32 + k * T:32 + (k + 1) * T]]
                for n, v in enumerate(vals):
                    ins = dve.tensor_tensor(hit_val[:, k, n, :].rearrange("p (a s) -> p a s", a=T),
                                            half.rearrange("p (a s) -> p a s", a=T),
                                            v.unsqueeze(2).to_broadcast([P, T, TAB]), ALU.mult)
                ins.then_inc(hits_ok, 1)
            slot_f = rt[:, 11, 0:TAB]
            started = rt[:, 0:4, :].rearrange("p a b -> p (a b)")[:, 0:TAB * E].rearrange("p (s e) -> p s e", e=E)
            link(dve.tensor_tensor(started, const("iota_slot").unsqueeze(2).to_broadcast([P, TAB, E]),
                                   v16(13).unsqueeze(1).to_broadcast([P, TAB, E]), ALU.is_ge))
            link(dve.tensor_reduce(slot_f, started, AX_X, ALU.add))
            link(dve.tensor_scalar(slot_f, slot_f, -1.0, None, ALU.add))
            link(dve.tensor_copy(slot_e[:, :], slot_f))
            link(dve.tensor_scalar(sel1_col[:, :], slot_f, const("is_bias1"), None, ALU.is_equal))
            link(dve.tensor_scalar(sel2_col[:, :], slot_f, const("is_bias2"), None, ALU.is_equal))
            new = rt[:, 11, 64:64 + TAB]
            not_last = rt[:, 11, 128:128 + TAB]
            link(dve.tensor_scalar(not_last, slot_f, float(E - 1), None, ALU.is_lt))
            link(dve.memset(new, 0.0))
            link(dve.tensor_tensor(new[:, 0:TAB - 1], slot_f[:, 1:TAB], slot_f[:, 0:TAB - 1], ALU.not_equal))
            link(dve.tensor_tensor(new[:, 0:TAB - 1], new[:, 0:TAB - 1], not_last[:, 1:TAB], ALU.mult))
            dve.memset(starts[:, 0:1], 1)
            link(dve.tensor_copy(starts[:, 1:TAB], new[:, 0:TAB - 1]))
            used = rt[:, 11, 192:193]
            link(dve.tensor_tensor(used, v16(13)[:, E - 1:E], v16(12)[:, E - 1:E], ALU.add))
            link(dve.tensor_scalar(used, used, 1.0, None, ALU.add))
            used_i = rt[:, 11, 193:194].bitcast(I32)
            link(dve.tensor_copy(used_i, used))
            link(dve.tensor_scalar(pairs[:, :], used_i, 1, None, ALU.arith_shift_right))
            split(0, 1, 2)
            dve.wait_ge(table_mm, 1)
            tab = ps[:, 2, 0:3 * TAB].rearrange("p (n s) -> p n s", n=3)
            dve.tensor_scalar(tok_i[:, :], tab[:, 0, :], -1.0, 0.0, ALU.add, ALU.max).then_inc(tok_ok, 1)
            link(dve.tensor_scalar(rt[:, 10, 0:TAB], tab[:, 0, :], 0.0, const("dump_row_1"), ALU.is_equal, ALU.mult))
            link(dve.scalar_tensor_tensor(scat_i[:, :], tab[:, 0, :], -1.0, rt[:, 10, 0:TAB], ALU.add, ALU.add))
            link(dve.tensor_copy(rt[:, 10, 128:128 + TAB], tab[:, 1, :]))
            dve.tensor_tensor(gate[:, :], rt[:, 10, 128:128 + TAB], tab[:, 2, :], ALU.add).then_inc(table_ok, 1)
            split(1, 0, 1)

            def slot_x_lo(s, par):
                dve.wait_ge(x_hi_ok, s + 1)
                dve.tensor_tensor(xt_lo[:, par, :], xt_ps(par), xt_hi[:, par, :].bitcast(F32), ALU.subtract).then_inc(x_lo_ok, 1)

            def slot_stats(s, par):
                dve.wait_ge(mm1, s + 1)
                link(dve.bn_stats(h_stats[:, par, :], h_ps(par)))
                dve.sem_inc(dve_turn, 1)
                dve.bn_aggr(h_mv[:, par, :], h_stats[:, par, :]).then_inc(h_var, 1)

            def split_next(n, e, start):
                with dve.If(start == 1):
                    at = bass.ds(((e + 1) & 1) * (C * D), C * D)
                    dve.wait_ge(split_hi[n], e + 2)
                    dve.tensor_tensor(w_lo[:, n, at], w_raw[:, n, :, :].rearrange("p a n -> p (a n)")[:, at],
                                      w_hi[:, n, at].bitcast(F32), ALU.subtract).then_inc(split_lo[n], 1)

            e_1 = dve.value_load(slot_e[0:1, 1:2], min_val=0, max_val=E - 1)
            start_1 = dve.value_load(starts[0:1, 1:2], min_val=0, max_val=1)
            live = dve.value_load(pairs[0:1, 0:1], min_val=1, max_val=SLOTS // 2)
            slot_x_lo(0, 0)
            slot_x_lo(1, 1)
            slot_stats(0, 0)
            slot_x_lo(2, 0)
            slot_stats(1, 1)
            split_next(0, e_1, start_1)
            dve.sem_inc(y_ok, 2)
            with dve.Fori(0, SLOTS // 2) as j:
                with dve.If(j < live):
                    own.enter(j, 2)
                    for par in range(2):
                        s = j * 2 + par
                        e_s = dve.value_load(slot_e[0:1, bass.ds(s, 1)], min_val=0, max_val=E - 1)
                        e_a = dve.value_load(slot_e[0:1, bass.ds(s + 2, 1)], min_val=0, max_val=E - 1)
                        start_s = dve.value_load(starts[0:1, bass.ds(s, 1)], min_val=0, max_val=1)
                        start_a = dve.value_load(starts[0:1, bass.ds(s + 2, 1)], min_val=0, max_val=1)
                        dve.wait_ge(g_hi_ok, s + 1)
                        dve.tensor_tensor(gt_lo[:, par, :], g_sb[:, par, :], gt_hi[:, par, :].bitcast(F32),
                                          ALU.subtract).then_inc(g_lo_ok, 1)
                        slot_x_lo(s + 3, 1 - par)
                        slot_stats(s + 2, par)
                        split_next(0, e_a, start_a)
                        split_next(1, e_s, start_s)
                        dve.wait_ge(mm2, s + 1)
                        dve.wait_ge(scattered, s * 16 + 16)
                        dve.tensor_scalar(y_sb[:, par, :], y_ps(par), gate[:, bass.ds(s, 1)], None, ALU.mult).then_inc(y_ok, 1)
                    own.leave(0)

        @block.tensor
        def _(pe):
            ident = const("ident")
            ones = const("ones")
            pe.wait_ge(consts_in, 16)
            for i, col in ((0, 8), (1, 15)):
                pe.wait_ge(w_means, i + 1)
                pe.matmul(side_bank(0, i)[:, 0:1], ones, small[:, col:col + 1], start=True, stop=True).then_inc(w_sums, 1)

            def transpose_x(t, par):
                pe.wait_ge(xq_ready, t + 1)
                for c in range(C):
                    ins = pe.transpose(side_bank(0, par)[:, c * P:(c + 1) * P], xq[:, par, c * P:(c + 1) * P], ident)
                ins.then_inc(xq_t, 1)

            def support(t, par):
                pe.wait_ge(xq_lo_ok, t + 1)
                for part in (xq_hi, xq_lo):
                    for c in range(C):
                        ins = pe.matmul(side_bank(0, 2 + par), part[:, par, c * P:(c + 1) * P],
                                        w_int[:, c * D:(c + 1) * D],
                                        start=part is xq_hi and c == 0, stop=part is xq_lo and c == C - 1)
                ins.then_inc(sup_mm, 1)

            sup_flat = sup[:, :, :].rearrange("p t d -> p (t d)")

            def step(q, m, par, n, first=False, last=False):
                pe.wait_ge(adj_lo_ok, n)
                for k in range(2):
                    for i in range(TQ):
                        for part in (adj_hi, adj_lo):
                            ins = pe.matmul(acc_bank(q, i), part[:, par, k, i * P:(i + 1) * P],
                                            sup_flat[:, bass.ds((m * 2 + k) * D, D)],
                                            start=first and k == 0 and part is adj_hi,
                                            stop=last and k == 1 and part is adj_lo)
                ins.then_inc(adj_mm, 1)

            pe.sem_inc(adj_mm, 1)
            pe.wait_ge(w_ready, 1)
            transpose_x(0, 0)
            transpose_x(1, 1)
            support(0, 0)
            transpose_x(2, 0)
            support(1, 1)
            pe.wait_ge(sup_ok, 2)
            step(0, 0, 0, 1, first=True)
            with pe.Fori(0, MID) as j:
                for half in range(2):
                    t = j * 4 + 2 * half
                    transpose_x(t + 3, 1)
                    support(t + 2, 0)
                    transpose_x(t + 4, 0)
                    support(t + 3, 1)
                    pe.wait_ge(sup_ok, t + 4)
                    step(0, j * 2 + (1 + half), 1 - half, j * 2 + (2 + half))
            transpose_x(T - 1, 1)
            support(T - 2, 0)
            support(T - 1, 1)
            pe.wait_ge(sup_ok, T)
            step(0, STEPS - 1, 1, STEPS, last=True)

            def finish_t(t):
                pe.wait_ge(xn_ok, t + 1)
                if t >= 2:
                    pe.wait_ge(xn_t_ok, t - 1)
                for c in range(C):
                    ins = pe.transpose(side_bank(t // TQ + 1, t % 2)[:, c * P:(c + 1) * P],
                                       xn[:, t % 2, c * P:(c + 1) * P], ident)
                ins.then_inc(xn_tp, 1)

            def router(t):
                pe.wait_ge(xn_t_ok, t + 1)
                if t >= 2:
                    pe.wait_ge(logits_ok, t - 1)
                for c in range(C):
                    ins = pe.matmul(side_bank(t // TQ + 1, 2 + t % 2)[:, 0:E], xn_t[:, t % 2, c * P:(c + 1) * P],
                                    wr_sb[:, c * E:(c + 1) * E], start=c == 0, stop=c == C - 1)
                ins.then_inc(router_mm, 1)

            pe.wait_ge(small_in, 64)
            for q in range(1, QUARTERS):
                t0 = TQ * (q - 1)
                if q > 1:
                    pe.wait_ge(logits_ok, t0)
                n = STEPS * q + 1
                step(q, 0, 0, n, first=True)
                for jj in range(MID):
                    if jj == 0:
                        pe.wait_ge(acc_read, t0 + TQ)
                    finish_t(t0 + jj)
                    step(q, 2 * jj + 1, 1, n + 2 * jj + 1)
                    router(t0 + jj)
                    step(q, 2 * jj + 2, 0, n + 2 * jj + 2)
                finish_t(t0 + MID)
                step(q, STEPS - 1, 1, STEPS * (q + 1), last=True)
                router(t0 + MID)
            pe.wait_ge(acc_read, T)
            for t in range(T - TQ, T):
                finish_t(t)
                if t > T - TQ:
                    router(t - 1)
            router(T - 1)

            pe.wait_ge(picked, 1)
            chosen = rt[:, 7, :]
            pe.matmul(ps[:, 0, 0:E * T], const("tri"), chosen, start=True, stop=True)
            pe.matmul(ps[:, 1, 0:E * T], ones, chosen, start=True, stop=True).then_inc(ranks, 1)
            for k in range(TOP):
                pe.wait_ge(hits_ok, k + 1)
                for t in range(T):
                    ins = pe.matmul(ps[:, 2, 0:3 * TAB].rearrange("p (n s) -> p n s", n=3), hit_row[:, k * T + t, :],
                                    hit_val[:, k, :, t * TAB:(t + 1) * TAB],
                                    start=k == 0 and t == 0, stop=k == TOP - 1 and t == T - 1)
            ins.then_inc(table_mm, 1)

            def rows_t(s, par, landed):
                pe.wait_ge(gathered[par], landed)
                for c in range(C):
                    ins = pe.transpose(xt_ps(par)[:, c * P:(c + 1) * P], xg[:, par, c * P:(c + 1) * P], ident)
                ins.then_inc(x_tp, 1)

            def layer(dst, n, par, e, act_hi, act_lo, sel, done):
                pe.matmul(dst, sel[:, par, :], bias_sb[:, :], start=True, stop=False)
                for c in range(C):
                    at = bass.ds((e & 1) * (C * D) + c * D, D)
                    pe.matmul(dst, act_hi[:, par, c * P:(c + 1) * P], w_hi[:, n, at], start=False, stop=False)
                    pe.matmul(dst, act_lo[:, par, c * P:(c + 1) * P], w_hi[:, n, at], start=False, stop=False)
                    ins = pe.matmul(dst, act_hi[:, par, c * P:(c + 1) * P], w_lo[:, n, at], start=False, stop=c == C - 1)
                ins.then_inc(done, 1)

            pe.wait_ge(table_ok, 1)
            rows_t(0, 0, 16)
            rows_t(1, 1, 16)
            e_1 = pe.value_load(slot_e[0:1, 1:2], min_val=0, max_val=E - 1)
            live = pe.value_load(pairs[0:1, 0:1], min_val=1, max_val=SLOTS // 2)
            pe.wait_ge(x_lo_ok, 1)
            pe.wait_ge(split_lo[0], 1)
            pe.wait_ge(sel_ok, 3)
            pe.wait_ge(bias_ok, 1)
            layer(h_ps(0), 0, 0, 0, xt_hi, xt_lo, sel1, mm1)
            rows_t(2, 0, 32)
            pe.wait_ge(x_lo_ok, 2)
            pe.wait_ge(split_lo[0], e_1 + 1)
            layer(h_ps(1), 0, 1, e_1, xt_hi, xt_lo, sel1, mm1)
            with pe.Fori(0, SLOTS // 2) as j:
                with pe.If(j < live):
                    for par in range(2):
                        s = j * 2 + par
                        e_s = pe.value_load(slot_e[0:1, bass.ds(s, 1)], min_val=0, max_val=E - 1)
                        e_a = pe.value_load(slot_e[0:1, bass.ds(s + 2, 1)], min_val=0, max_val=E - 1)
                        pe.wait_ge(h_hat_ok, s + 1)
                        for c in range(C):
                            ins = pe.transpose(ht_ps(par)[:, c * P:(c + 1) * P], h_hat[:, par, c * P:(c + 1) * P], ident)
                        ins.then_inc(h_tp, 1)
                        rows_t(s + 3, 1 - par, j * 16 + (32 + 16 * par))
                        pe.wait_ge(x_lo_ok, s + 3)
                        pe.wait_ge(split_lo[0], e_a + 1)
                        pe.wait_ge(sel_ok, s * 2 + 4)
                        layer(h_ps(par), 0, par, e_a, xt_hi, xt_lo, sel1, mm1)
                        pe.wait_ge(g_lo_ok, s + 1)
                        pe.wait_ge(split_lo[1], e_s + 1)
                        pe.wait_ge(y_ok, s + 1)
                        layer(y_ps(par), 1, par, e_s, gt_hi, gt_lo, sel2, mm2)


_OUT_ROWS = N + P


def kernel(x, adj, L0_gnn_adj_scaling_factor, L0_gnn_weight, L0_gnn_wgt_alpha, L0_gnn_act_alpha, L0_gnn_act_alpha2,
           L0_ffn_Wr, L0_ffn_br, L0_ffn_W1, L0_ffn_b1, L0_ffn_g1, L0_ffn_be1, L0_ffn_W2, L0_ffn_b2):
    import concourse.bacc as bacc
    from concourse.bass_utils import run_bass_kernel_spmd

    def chunked(w):
        w = np.asarray(w)
        w = w.reshape(-1, C, P, w.shape[-1]).transpose(0, 2, 1, 3)
        return np.ascontiguousarray(w.reshape(-1, C * w.shape[-1]))

    def rows(v):
        return np.ascontiguousarray(np.broadcast_to(v, (P, v.size)))

    scalars = np.stack([np.asarray(v).reshape(()) for v in
                        (L0_gnn_adj_scaling_factor, L0_gnn_wgt_alpha, L0_gnn_act_alpha, L0_gnn_act_alpha2)])
    by_hidden = [np.ascontiguousarray(np.asarray(v).reshape(E * C, P).T) for v in (L0_ffn_g1, L0_ffn_be1)]
    ins = {
        "x": np.asarray(x),
        "adj_t": np.ascontiguousarray(np.asarray(adj).T),
        "gnn_w": chunked(L0_gnn_weight),
        "scalars": rows(scalars),
        "wr": chunked(L0_ffn_Wr),
        "br": rows(np.asarray(L0_ffn_br)),
        "w1": chunked(L0_ffn_W1),
        "b1": np.asarray(L0_ffn_b1),
        "g1": by_hidden[0],
        "be1": by_hidden[1],
        "w2": chunked(L0_ffn_W2),
        "b2": np.asarray(L0_ffn_b2),
        "consts": constants(),
    }
    nc = bacc.Bacc("TRN2", target_bir_lowering=False, num_devices=1)
    aps = {n: nc.dram_tensor(f"in_{n}", a.shape, mybir.dt.from_np(a.dtype), kind="ExternalInput").ap()
           for n, a in ins.items()}
    xn_rows = nc.dram_tensor("xn_rows", [N, D], F32, kind="Internal").ap()
    out = nc.dram_tensor("out", [_OUT_ROWS, D], F32, kind="ExternalOutput").ap()
    gnn_moe_program(nc, xn_rows=xn_rows, out=out, **aps)
    r = run_bass_kernel_spmd(nc, [{f"in_{n}": a for n, a in ins.items()}], core_ids=[0])
    return r.results[0]["out"][:N]
```

```python
from contextlib import ExitStack

import numpy as np

import concourse.bass as bass
from concourse import mybir

ALU = mybir.AluOpType
ACT = mybir.ActivationFunctionType
F32 = mybir.dt.float32
F32R = mybir.dt.float32r
I32 = mybir.dt.int32
AX_X = mybir.AxisListType.X

P = 128
N = 2048
D = 512
E = 16
T = N // P
C = D // P
TOP = 2
SLOTS = (TOP * N - E) // P + E
SLOTS += SLOTS % 2
TAB = SLOTS + 6
QUARTERS = 4
TQ = T // QUARTERS
STEPS = T // 2
LN_EPS = 1e-5
MAGIC = 1.5 * 2.0 ** 23
N_ACT = 15.0
N_WGT = 7.0

_WIDTHS = [("ident", P), ("tri", P), ("ones", P), ("iota_row", P), ("iota_slot", TAB), ("iota_e", E),
           ("full_tiles", E), ("token_1", T), ("is_bias1", 1), ("is_bias2", 1), ("dump_row_1", 1),
           ("scan_keep", E * T), ("neg_half", 1), ("minus_one", 1)]
COLS, _at = {}, 0
for _name, _w in _WIDTHS:
    COLS[_name] = (_at, _at + _w)
    _at += _w
CONSTS = _at


def constants():
    k = np.zeros((P, CONSTS), np.float32)
    p = np.arange(P)

    def put(name, v):
        a, b = COLS[name]
        k[:, a:b] = v

    put("ident", np.eye(P))
    put("tri", p[:, None] < p[None, :])
    put("ones", 1.0)
    put("iota_row", p[None, :])
    put("iota_slot", np.arange(TAB)[None, :])
    put("iota_e", np.arange(E)[None, :])
    put("full_tiles", P * np.arange(E)[None, :])
    put("token_1", P * np.arange(T)[None, :] + p[:, None] + 1)
    put("is_bias1", np.where(p < 64, p % 32, 1000)[:, None])
    put("is_bias2", np.where(p >= 64, p % 32, 1000)[:, None])
    put("dump_row_1", (N + p + 1)[:, None])
    put("scan_keep", np.tile((np.arange(T) > 0).astype(np.float32), E)[None, :])
    put("neg_half", -0.5)
    put("minus_one", -1.0)
    return k


class Chain:

    def __init__(self, eng, sem):
        self.eng, self.sem = eng, sem
        self.base, self.n, self.i, self.per = 0, 0, None, 0

    def link(self, ins):
        self.need(self.mark(ins))

    def mark(self, ins):
        self.n += 1
        ins.then_inc(self.sem, 1)
        return self.base + self.n

    def need(self, at):
        self.eng.wait_ge(self.sem, at if self.i is None else self.i * self.per + at)

    def enter(self, i, per):
        self.base, self.n, self.i, self.per = self.base + self.n, 0, i, per

    def leave(self, trips):
        assert self.n == self.per, (self.n, self.per)
        self.base, self.n, self.i = self.base + trips * self.per, 0, None


def gnn_moe_program(nc, x, adj_t, gnn_w, scalars, wr, br, w1, b1, g1, be1, w2, b2, consts, xn_rows, out):
    with ExitStack() as ctx:
        usable = nc.sbuf_usable_end
        first = (nc.sbuf_base + 31) // 32 * 32
        where = [first]

        def place(name, shape, dt):
            size = int(np.prod(shape[1:])) * 4
            t = nc.alloc_sbuf_tensor_at(name, shape, dt, offset=where[0])
            where[0] += (size + 31) // 32 * 32
            assert where[0] <= usable, (name, where[0], usable)
            return t

        def sem(name):
            return ctx.enter_context(nc.semaphore(name))

        k_sb = place("k_sb", [P, CONSTS], F32)
        sc = place("sc", [P, 4], F32)
        g1_sb = place("g1_sb", [P, E * C], F32)
        be1_sb = place("be1_sb", [P, E * C], F32)
        br_sb = place("br_sb", [P, E], F32)
        wr_sb = place("wr_sb", [P, C * E], F32)
        bias_sb = place("bias_sb", [P, D], F32R)
        w_raw = place("w_raw", [P, 2, 2, C * D], F32)
        logits = place("logits", [P, T, E], F32)
        small = place("small", [P, 64], F32)
        stats = place("stats", [P, 4, 6], F32)
        mv = place("mv", [P, T, 2], F32)
        rstd = place("rstd", [P, T, 2], F32)
        tok_i = place("tok_i", [P, TAB], I32)
        scat_i = place("scat_i", [P, TAB], I32)
        gate = place("gate", [P, TAB + 1], F32)
        sel1_col = place("sel1_col", [P, TAB], F32)
        sel2_col = place("sel2_col", [P, TAB], F32)
        plan = place("plan", [P, SLOTS // 2], I32)
        pairs = place("pairs", [P, 1], I32)
        end_fixed = where[0]

        sup = place("sup", [P, T, D], F32R)
        adj_raw = place("adj_raw", [P, 2, 2, D], F32)
        adj_hi = place("adj_hi", [P, 2, 2, D], F32R)
        adj_lo = place("adj_lo", [P, 2, 2, D], F32R)
        xq = place("xq", [P, 2, D], F32)
        xq_hi = place("xq_hi", [P, 2, D], F32R)
        xq_lo = place("xq_lo", [P, 2, D], F32R)
        end_adj = where[0]
        w_int = place("w_int", [P, C * D], F32R)
        x_sb = place("x_sb", [P, T, D], F32)
        xn = place("xn", [P, 2, D], F32)
        xn_t = place("xn_t", [P, 2, D], F32)
        gw_raw = place("gw_raw", [P, C * D], F32)
        relu_sb = place("relu_sb", [P, 2, D], F32)
        rt = place("rt", [P, 14, E * T], F32)
        rv = place("rv", [P, 16, 32], F32)
        b_raw = place("b_raw", [P, D], F32)
        b_hi = place("b_hi", [P, D], F32R)
        end_gnn = where[0]

        where[0] = end_fixed
        w_hi = place("w_hi", [P, 2, 2 * C * D], F32R)
        w_lo = place("w_lo", [P, 2, 2 * C * D], F32R)
        end_w = where[0]
        where[0] = max(end_w, end_adj)
        ffn0 = where[0]
        xg = place("xg", [P, 2, D], F32)
        xt_hi = place("xt_hi", [P, 2, D], F32R)
        xt_lo = place("xt_lo", [P, 2, D], F32R)
        h_hat = place("h_hat", [P, 2, D], F32)
        g_sb = place("g_sb", [P, 2, D], F32)
        gt_hi = place("gt_hi", [P, 2, D], F32R)
        gt_lo = place("gt_lo", [P, 2, D], F32R)
        y_sb = place("y_sb", [P, 2, D], F32)
        sel1 = place("sel1", [P, 2, P], F32R)
        sel2 = place("sel2", [P, 2, P], F32R)
        idx_g = place("idx_g", [P, 2], I32)
        idx_s = place("idx_s", [P, 2], I32)
        h_stats = place("h_stats", [P, 2, 6], F32)
        h_mv = place("h_mv", [P, 2, 2], F32)
        h_rs = place("h_rs", [P, 2, 4], F32)
        hit_row_at = where[0]
        hit_row = place("hit_row", [P, TOP * T, P], F32R)
        assert where[0] <= end_gnn
        where[0] = ffn0
        hit_slot = place("hit_slot", [P, TOP * T * TAB], F32)
        hit_val = place("hit_val", [P, TOP, 3, T * TAB], F32R)
        assert where[0] <= hit_row_at

        ps = ctx.enter_context(nc.psum_tensor("ps", [P, 8, D], F32))

        def const(name):
            a, b = COLS[name]
            return k_sb[:, a:b]

        pos_row = rt[:, 12, 128:160]

        consts_in = sem("consts_in")
        scalars_in = sem("scalars_in")
        small_in = sem("small_in")
        gw_in = sem("gw_in")
        x_in = [sem(f"x_in{i}") for i in range(4)]
        adj_in = [sem(f"adj_in{i}") for i in range(2)]
        dve_own = sem("dve_own")
        pool_own = sem("pool_own")
        pool_turn = sem("pool_turn")
        dve_turn = sem("dve_turn")
        w_means = sem("w_means")
        w_sums = sem("w_sums")
        w_var = sem("w_var")
        w_rstd = sem("w_rstd")
        w_ready = sem("w_ready")
        x_var = sem("x_var")
        x_rstd = sem("x_rstd")
        xq_ready = sem("xq_ready")
        xq_t = sem("xq_t")
        xq_hi_ok = sem("xq_hi_ok")
        xq_lo_ok = sem("xq_lo_ok")
        sup_mm = sem("sup_mm")
        relu_ok = sem("relu_ok")
        sup_round = sem("sup_round")
        sup_ok = sem("sup_ok")
        adj_hi_ok = sem("adj_hi_ok")
        adj_lo_ok = sem("adj_lo_ok")
        adj_mm = sem("adj_mm")
        acc_read = sem("acc_read")
        mid_ok = sem("mid_ok")
        mid_rstd = sem("mid_rstd")
        xn_ok = sem("xn_ok")
        xn_tp = sem("xn_tp")
        xn_t_ok = sem("xn_t_ok")
        router_mm = sem("router_mm")
        logits_ok = sem("logits_ok")
        mid_out = [sem(f"mid_out{i}") for i in range(2)]
        bias_in = sem("bias_in")
        bias_ok = sem("bias_ok")
        exp_in = sem("exp_in")
        exp_ok = sem("exp_ok")
        picked = sem("picked")
        ranks = sem("ranks")
        tok_ok = sem("tok_ok")
        hits_ok = sem("hits_ok")
        table_mm = sem("table_mm")
        table_ok = sem("table_ok")
        raw_in = [sem(f"raw{n}_in") for n in (1, 2)]
        split_hi = [sem(f"split{n}_hi") for n in (1, 2)]
        split_lo = [sem(f"split{n}_lo") for n in (1, 2)]
        gathered = [sem(f"gathered{i}") for i in range(2)]
        x_tp = sem("x_tp")
        x_hi_ok = sem("x_hi_ok")
        x_lo_ok = sem("x_lo_ok")
        sel_ok = sem("sel_ok")
        mm1 = sem("mm1")
        h_var = sem("h_var")
        h_rstd = sem("h_rstd")
        h_hat_ok = sem("h_hat_ok")
        h_tp = sem("h_tp")
        gelu_ok = sem("gelu_ok")
        g_hi_ok = sem("g_hi_ok")
        g_lo_ok = sem("g_lo_ok")
        mm2 = sem("mm2")
        y_ok = sem("y_ok")
        scattered = sem("scattered")

        block = ctx.enter_context(nc.Block())

        def acc_bank(q, i):
            return ps[:, 4 * (q % 2) + i, :]

        def side_bank(q, i):
            return ps[:, 4 * (1 - q % 2) + i, :]

        def xt_ps(par):
            return ps[:, par, :]

        def h_ps(par):
            return ps[:, 2 + par, :]

        def ht_ps(par):
            return ps[:, 4 + par, :]

        def y_ps(par):
            return ps[:, 6 + par, :]

        def load_plan(eng, j):
            return eng.value_load(plan[0:1, bass.ds(j, 1)], min_val=0, max_val=2 ** 20 - 1)

        def expert_in(word, i):
            return (word >> (4 * i)) & (E - 1)

        def starts_in(word, i):
            return (word >> (16 + i)) & 1

        MID = 3
        LOOP0, TRIPS0 = 2, (STEPS - 4) // 2

        @block.sync
        def _(sp):
            sp.dma_start(sc[:, :], scalars).then_inc(scalars_in, 16)
            sp.dma_start(gw_raw[:, :], gnn_w).then_inc(gw_in, 16)
            sp.dma_start(k_sb[:, :], consts).then_inc(consts_in, 16)
            for i in range(4):
                sp.dma_start(x_sb[:, 4 * i:4 * i + 4, :],
                             x[4 * i * P:(4 * i + 4) * P, :].rearrange("(t p) d -> p t d", p=P)).then_inc(x_in[i], 16)
            view = adj_t.rearrange("(s k p) n -> p s k n", p=P, k=2)

            def load_adj(q, m, par):
                return sp.dma_start(adj_raw[:, par, :, :],
                                    view[:, m:m + 1, :, q * D:(q + 1) * D].rearrange("p s k n -> p (s k) n")
                                    if isinstance(m, int) else
                                    view[:, bass.ds(m, 1), :, q * D:(q + 1) * D].rearrange("p s k n -> p (s k) n")
                                    ).then_inc(adj_in[par], 16)

            for q in range(QUARTERS):
                for par in range(2):
                    if q:
                        sp.wait_ge(adj_lo_ok, STEPS * q - 1 + par)
                    load_adj(q, par, par)
                with sp.Fori(1, STEPS // 2) as j:
                    for par in range(2):
                        sp.wait_ge(adj_lo_ok, j * 2 + (STEPS * q - 1 + par))
                        load_adj(q, j * 2 + par, par)
            w_dram = (w1, w2)
            HALF = C * D // 2
            for e in range(2):
                for h in range(2):
                    for n in range(2):
                        if e or h:
                            sp.wait_ge(raw_in[n], 32 * e + 16 * h)
                        sp.dma_start(w_raw[:, n, e, h * HALF:(h + 1) * HALF],
                                     w_dram[n][e * P:(e + 1) * P, h * HALF:(h + 1) * HALF]).then_inc(raw_in[n], 16)
            with sp.Fori(1, E // 2) as j:
                for par in range(2):
                    for h in range(2):
                        for n in range(2):
                            sp.wait_ge(raw_in[n], j * 64 + (32 * par + 16 * h))
                            if h == 0:
                                sp.wait_ge(split_lo[n], j * 2 + (par - 1))
                            sp.dma_start(w_raw[:, n, par, h * HALF:(h + 1) * HALF],
                                         w_dram[n][bass.ds(j * 2 * P + par * P, P), h * HALF:(h + 1) * HALF]
                                         ).then_inc(raw_in[n], 16)

        @block.gpsimd
        def _(pool):
            own = Chain(pool, pool_own)
            pool.dma_start(g1_sb[:, :], g1).then_inc(small_in, 16)
            pool.dma_start(be1_sb[:, :], be1).then_inc(small_in, 16)
            pool.dma_start(br_sb[:, :], br).then_inc(small_in, 16)
            pool.dma_start(wr_sb[:, :], wr).then_inc(small_in, 16)
            neg_half = const("neg_half")
            own.link(pool.memset(b_raw[:, :], 0.0))
            for base, b in ((0, b1), (32, b1), (64, b2), (96, b2)):
                pool.dma_start(b_raw[base:base + E, :], b).then_inc(bias_in, 16)
            neg_half = const("neg_half")
            pool.wait_ge(consts_in, 16)
            for h in range(2):
                pool.dma_start(out[N + h * P // 2:N + (h + 1) * P // 2, :], k_sb[h * P // 2:(h + 1) * P // 2, 0:D]
                               ).then_inc(scattered, 16)
            pool.wait_ge(w_var, 1)
            pool.tensor_tensor(small[:, 13:14], small[:, 12:13], neg_half, ALU.pow).then_inc(w_rstd, 1)
            pool.wait_ge(x_var, 1)
            pool.tensor_tensor(rstd[:, :, 0], rstd[:, :, 1], neg_half.to_broadcast([P, T]), ALU.pow).then_inc(x_rstd, 1)

            for t in range(T):
                pool.wait_ge(mid_ok, t + 1)
                own.link(pool.tensor_scalar(rstd[:, t, 1:2], mv[:, t, 1:2], LN_EPS, None, ALU.add))
                own.link(pool.tensor_tensor(rstd[:, t, 0:1], rstd[:, t, 1:2], neg_half, ALU.pow))
                own.link(pool.tensor_tensor(rstd[:, t, 1:2], mv[:, t, 0:1], rstd[:, t, 0:1], ALU.mult))
                pool.tensor_scalar(rstd[:, t, 1:2], rstd[:, t, 1:2], -1.0, None, ALU.mult).then_inc(mid_rstd, 1)

            def select(dst, par, col, s):
                return pool.tensor_copy(dst[:, par, :], col[:, bass.ds(s, 1)].to_broadcast([P, P]))

            def gather(par):
                return pool.indirect_dma_start(
                    xg[:, par, :], None, xn_rows,
                    bass.IndirectOffsetOnAxis(ap=idx_g[:, par:par + 1], axis=0)).then_inc(gathered[par], 16)

            def slot_rstd(par):
                own.link(pool.tensor_scalar(h_rs[:, par, 2:3], h_mv[:, par, 1:2], LN_EPS, None, ALU.add))
                own.link(pool.tensor_tensor(h_rs[:, par, 0:1], h_rs[:, par, 2:3], neg_half, ALU.pow))
                own.link(pool.tensor_tensor(h_rs[:, par, 3:4], h_mv[:, par, 0:1], h_rs[:, par, 0:1], ALU.mult))
                pool.tensor_tensor(h_rs[:, par, 1:2], h_rs[:, par, 3:4], const("minus_one"), ALU.mult).then_inc(h_rstd, 1)

            for i in range(2):
                pool.wait_ge(mid_out[i], 16 * T)
            pool.wait_ge(tok_ok, 1)
            for s in range(2):
                own.link(pool.tensor_copy(idx_g[:, s:s + 1], tok_i[:, s:s + 1]))
                gather(s)
            pool.wait_ge(table_ok, 1)
            pool.wait_ge(scattered, 32)
            select(sel1, 0, sel1_col, 0).then_inc(sel_ok, 1)
            select(sel1, 1, sel1_col, 1).then_inc(sel_ok, 1)
            select(sel2, 0, sel2_col, 0).then_inc(sel_ok, 1)
            for s in range(2, 5):
                pool.wait_ge(x_tp, s - 1)
                own.link(pool.tensor_copy(idx_g[:, s % 2:s % 2 + 1], tok_i[:, s:s + 1]))
                gather(s % 2)
                if s == 4:
                    select(sel1, 0, sel1_col, 2).then_inc(sel_ok, 1)
                if s >= 3:
                    pool.wait_ge(h_var, s - 2)
                    slot_rstd(s - 3)
            live = pool.value_load(pairs[0:1, 0:1], min_val=1, max_val=SLOTS // 2)
            with pool.Fori(0, SLOTS // 2) as j:
                with pool.If(j < live):
                    own.enter(j, 2 * 5)
                    for par in range(2):
                        s = j * 2 + par
                        pool.wait_ge(x_tp, s + 4)
                        pool.sem_inc(pool_turn, 1)
                        own.link(pool.tensor_copy(idx_g[:, 1 - par:2 - par], tok_i[:, bass.ds(s + 5, 1)]))
                        pool.sem_inc(pool_turn, 1)
                        gather(1 - par)
                        select(sel1, 1 - par, sel1_col, s + 3).then_inc(sel_ok, 1)
                        select(sel2, 1 - par, sel2_col, s + 1).then_inc(sel_ok, 1)
                        pool.wait_ge(h_var, s + 3)
                        pool.sem_inc(pool_turn, 1)
                        slot_rstd(par)
                        own.link(pool.tensor_copy(idx_s[:, par:par + 1], scat_i[:, bass.ds(s, 1)]))
                        pool.wait_ge(y_ok, s + 3)
                        pool.wait_ge(scattered, s * 16 + 32)
                        pool.sem_inc(pool_turn, 1)
                        pool.indirect_dma_start(
                            out, bass.IndirectOffsetOnAxis(ap=idx_s[:, par:par + 1], axis=0),
                            y_sb[:, par, :], None, compute_op=ALU.add).then_inc(scattered, 16)
                    own.leave(0)
            pool.wait_ge(scattered, live * 32 + 32)
            for par in range(2):
                pool.wait_ge(gathered[par], live * 16 + 16 * (3 - par))

        @block.scalar
        def _(act):
            def hi_step(par, arrived, before):
                act.wait_ge(adj_in[par], arrived)
                if before is not None:
                    act.wait_ge(adj_mm, before + 1)
                act.activation(adj_hi[:, par, :, :], adj_raw[:, par, :, :], ACT.Copy, scale=small[:, 0:1]).then_inc(adj_hi_ok, 1)

            def g_hi(t, par):
                act.wait_ge(xq_t, t + 1)
                act.activation(xq_hi[:, par, :], side_bank(0, par), ACT.Copy, bias=-MAGIC).then_inc(xq_hi_ok, 1)

            def g_relu(t, par):
                act.wait_ge(sup_mm, t + 1)
                if not isinstance(t, int) or t >= 2:
                    act.wait_ge(sup_ok, t - 1)
                act.activation(relu_sb[:, par, :], side_bank(0, 2 + par), ACT.Relu, scale=small[:, 5:6]).then_inc(relu_ok, 1)

            def finish_xn(t):
                act.wait_ge(mid_rstd, t + 1)
                if t >= 2:
                    act.wait_ge(xn_tp, t - 1)
                    act.wait_ge(mid_out[t % 2], 32 * (t // 2))
                act.activation(xn[:, t % 2, :], x_sb[:, t, :], ACT.Identity, scale=rstd[:, t, 0:1],
                               bias=rstd[:, t, 1:2]).then_inc(xn_ok, 1)
                act.dma_start(out[t * P:(t + 1) * P, :], x_sb[:, t, :]).then_inc(mid_out[t % 2], 16)
                act.wait_ge(xn_ok, t + 1)
                act.dma_start(xn_rows[t * P:(t + 1) * P, :], xn[:, t % 2, :]).then_inc(mid_out[t % 2], 16)

            def finish_t(t):
                act.wait_ge(xn_tp, t + 1)
                act.activation(xn_t[:, t % 2, :], side_bank(t // TQ + 1, t % 2), ACT.Copy).then_inc(xn_t_ok, 1)

            def g_sup(t, par):
                act.wait_ge(sup_round, t + 1)
                act.activation(sup[:, :, :].rearrange("p t d -> p (t d)")[:, bass.ds(t * D, D)], relu_sb[:, par, :],
                               ACT.Copy, bias=-MAGIC).then_inc(sup_ok, 1)

            def pair(m, par):
                more = not (isinstance(m, int) and m == STEPS - 1)
                g_relu(m * 2, 0)
                if more:
                    g_hi(m * 2 + 2, 0)
                arrived = m * 8 + (16 - 8 * par)
                hi_step(par, arrived, None if isinstance(m, int) and m < 2 else m - 1)
                g_relu(m * 2 + 1, 1)
                if more:
                    g_hi(m * 2 + 3, 1)
                g_sup(m * 2, 0)
                g_sup(m * 2 + 1, 1)

            act.wait_ge(w_ready, 1)
            g_hi(0, 0)
            g_hi(1, 1)
            for m in range(LOOP0):
                pair(m, m % 2)
            with act.Fori(0, TRIPS0) as j:
                for par in range(2):
                    pair(j * 2 + (LOOP0 + par), par)
            for m in range(LOOP0 + 2 * TRIPS0, STEPS):
                pair(m, m % 2)
            for q in range(1, QUARTERS):
                t0 = TQ * (q - 1)
                in0 = 16 * (STEPS // 2) * q
                hi_step(0, in0 + 16, STEPS * q - 1)
                for jj in range(MID):
                    hi_step(1, in0 + 16 * (jj + 1), STEPS * q + 2 * jj)
                    finish_xn(t0 + jj)
                    hi_step(0, in0 + 16 * (jj + 2), STEPS * q + 2 * jj + 1)
                    finish_t(t0 + jj)
                hi_step(1, in0 + 16 * (STEPS // 2), STEPS * (q + 1) - 2)
                finish_xn(t0 + MID)
                finish_t(t0 + MID)
            def split(n, par, arrived):
                act.wait_ge(raw_in[n], arrived)
                act.activation(w_hi[:, n, par * C * D:(par + 1) * C * D], w_raw[:, n, par, :], ACT.Copy).then_inc(split_hi[n], 1)

            act.wait_ge(adj_mm, STEPS * QUARTERS + 1)
            act.wait_ge(small_in, 64)
            split(0, 0, 32)
            for t in range(T - TQ, T):
                finish_xn(t)
                if t > T - TQ:
                    finish_t(t - 1)
            finish_t(T - 1)
            split(0, 1, 64)
            split(1, 0, 32)
            act.wait_ge(exp_in, 1)
            act.activation(rt[:, 1, :], rt[:, 0, :], ACT.Exp).then_inc(exp_ok, 1)

            def slot_x_hi(s, par):
                act.wait_ge(x_tp, s + 1)
                act.activation(xt_hi[:, par, :], xt_ps(par), ACT.Copy).then_inc(x_hi_ok, 1)

            def slot_h_hat(s, par):
                act.wait_ge(h_rstd, s + 1)
                act.activation(h_hat[:, par, :], h_ps(par), ACT.Identity, scale=h_rs[:, par, 0:1],
                               bias=h_rs[:, par, 1:2]).then_inc(h_hat_ok, 1)

            def split_next(n, e, start):
                with act.If(start == 1):
                    at = bass.ds(((e + 1) & 1) * (C * D), C * D)
                    act.wait_ge(raw_in[n], e * 32 + 64)
                    act.activation(w_hi[:, n, at], w_raw[:, n, :, :].rearrange("p a n -> p (a n)")[:, at],
                                   ACT.Copy).then_inc(split_hi[n], 1)

            act.wait_ge(exp_ok, 1)
            act.preload_act_table(ACT.Gelu)
            act.wait_ge(table_ok, 1)
            word = load_plan(act, 0)
            live = act.value_load(pairs[0:1, 0:1], min_val=1, max_val=SLOTS // 2)
            slot_x_hi(0, 0)
            slot_x_hi(1, 1)
            slot_h_hat(0, 0)
            slot_x_hi(2, 0)
            split_next(0, expert_in(word, 1), starts_in(word, 1))
            with act.Fori(0, SLOTS // 2) as j:
                with act.If(j < live):
                    word = load_plan(act, j)
                    for par in range(2):
                        s = j * 2 + par
                        e_s, e_a = expert_in(word, par), expert_in(word, par + 2)
                        act.wait_ge(h_tp, s + 1)
                        for c in range(C):
                            ins = act.activation(g_sb[:, par, c * P:(c + 1) * P], ht_ps(par)[:, c * P:(c + 1) * P],
                                                 ACT.Gelu, scale=g1_sb[:, bass.ds(e_s * C + c, 1)],
                                                 bias=be1_sb[:, bass.ds(e_s * C + c, 1)])
                        ins.then_inc(gelu_ok, 1)
                        act.wait_ge(gelu_ok, s + 1)
                        act.activation(gt_hi[:, par, :], g_sb[:, par, :], ACT.Copy).then_inc(g_hi_ok, 1)
                        slot_h_hat(s + 1, 1 - par)
                        slot_x_hi(s + 3, 1 - par)
                        split_next(0, e_a, starts_in(word, par + 2))
                        split_next(1, e_s, starts_in(word, par))

        @block.vector
        def _(dve):
            own = Chain(dve, dve_own)
            link = own.link
            dve.wait_ge(scalars_in, 16)

            link(dve.reciprocal(small[:, 0:4], sc[:, 0:4]))
            link(dve.tensor_scalar(small[:, 4:5], sc[:, 0:1], sc[:, 3:4], 1.0 / N_ACT, ALU.mult, ALU.mult))
            link(dve.tensor_scalar(small[:, 6:7], sc[:, 2:3], 1.0 / N_ACT, None, ALU.mult))
            link(dve.tensor_scalar(small[:, 7:8], sc[:, 1:2], 1.0 / N_WGT, None, ALU.mult))
            link(dve.tensor_tensor(small[:, 5:6], small[:, 6:7], small[:, 7:8], ALU.mult))

            dve.wait_ge(gw_in, 16)
            for c in range(C):
                ins = dve.bn_stats(stats[:, c, :], gw_raw[:, c * D:(c + 1) * D])
            link(ins)
            dve.bn_aggr(small[:, 8:10], stats[:, :, :].rearrange("p a b -> p (a b)")).then_inc(w_means, 1)
            dve.wait_ge(w_sums, 1)
            link(dve.tensor_scalar(small[:, 10:11], side_bank(0, 0)[:, 0:1], 1.0 / P, None, ALU.mult))
            link(dve.tensor_tensor(small[:, 11:12], small[:, 8:9], small[:, 10:11], ALU.subtract))
            link(dve.tensor_tensor(small[:, 14:15], small[:, 11:12], small[:, 11:12], ALU.mult))
            dve.tensor_tensor(small[:, 15:16], small[:, 14:15], small[:, 9:10], ALU.add).then_inc(w_means, 1)
            dve.wait_ge(w_sums, 2)
            dve.tensor_scalar(small[:, 12:13], side_bank(0, 1)[:, 0:1], D * D / (D * D - 1.0) / P, None,
                              ALU.mult).then_inc(w_var, 1)
            for t in range(T):
                if t % 4 == 0:
                    dve.wait_ge(x_in[t // 4], 16)
                ins = dve.bn_stats(stats[:, t % 4, :], x_sb[:, t, :])
                if t % 4 == 3:
                    link(ins)
                    for u in range(4):
                        ins = dve.bn_aggr(mv[:, t - 3 + u, :], stats[:, u, :])
                    link(ins)
            dve.tensor_scalar(rstd[:, :, 1], mv[:, :, 1], LN_EPS, None, ALU.add).then_inc(x_var, 1)
            dve.wait_ge(w_rstd, 1)
            link(dve.tensor_scalar(gw_raw[:, :], gw_raw[:, :], small[:, 10:11], small[:, 13:14], ALU.subtract, ALU.mult))
            link(dve.tensor_scalar(gw_raw[:, :], gw_raw[:, :], small[:, 1:2], 1.0, ALU.mult, ALU.min))
            link(dve.tensor_scalar(gw_raw[:, :], gw_raw[:, :], -1.0, N_WGT, ALU.max, ALU.mult))
            dve.tensor_scalar(w_int[:, :], gw_raw[:, :], MAGIC, MAGIC, ALU.add, ALU.subtract).then_inc(w_ready, 1)
            dve.wait_ge(x_rstd, 1)

            def x_tile(t):
                return x_sb[:, :, :].rearrange("p t d -> p (t d)")[:, bass.ds(t * D, D)]

            def sup_tile(t):
                return sup[:, :, :].rearrange("p t d -> p (t d)")[:, bass.ds(t * D, D)]

            def mean_of(t):
                return mv[:, :, :].rearrange("p t d -> p (t d)")[:, bass.ds(t * 2, 1)]

            def rstd_of(t):
                return rstd[:, :, :].rearrange("p t d -> p (t d)")[:, bass.ds(t * 2, 1)]

            def norm_x(t, par):
                return dve.tensor_scalar(xq[:, par, :], x_tile(t), mean_of(t), rstd_of(t), ALU.subtract, ALU.mult)

            def limit_x(par):
                return dve.tensor_scalar(xq[:, par, :], xq[:, par, :], small[:, 2:3], 1.0, ALU.mult, ALU.min)

            def round_x(par):
                dve.tensor_scalar(xq[:, par, :], xq[:, par, :], N_ACT, MAGIC, ALU.mult, ALU.add).then_inc(xq_ready, 1)

            def x_lo(t, par):
                dve.wait_ge(xq_hi_ok, t + 1)
                dve.scalar_tensor_tensor(xq_lo[:, par, :], side_bank(0, par), MAGIC, xq_hi[:, par, :].bitcast(F32),
                                         ALU.subtract, ALU.subtract).then_inc(xq_lo_ok, 1)

            def limit_sup(t, par):
                dve.wait_ge(relu_ok, t + 1)
                return dve.tensor_scalar(relu_sb[:, par, :], relu_sb[:, par, :], small[:, 3:4], 1.0, ALU.mult, ALU.min)

            def round_sup(par):
                dve.tensor_scalar(relu_sb[:, par, :], relu_sb[:, par, :], N_ACT, MAGIC, ALU.mult, ALU.add
                                  ).then_inc(sup_round, 1)

            def lo_step(par, n):
                dve.wait_ge(adj_hi_ok, n)
                dve.scalar_tensor_tensor(adj_lo[:, par, :, :].rearrange("p a b -> p (a b)"),
                                         adj_raw[:, par, :, :].rearrange("p a b -> p (a b)"), small[:, 0:1],
                                         adj_hi[:, par, :, :].rearrange("p a b -> p (a b)").bitcast(F32),
                                         ALU.mult, ALU.subtract).then_inc(adj_lo_ok, 1)

            def pair(m, par):
                known = isinstance(m, int)
                more_lo = not (known and m >= STEPS - 1)
                more_x = not (known and m >= STEPS - 2)
                limited = own.mark(limit_sup(m * 2, 0))
                if more_lo:
                    x_lo(m * 2 + 2, 0)
                own.need(limited)
                round_sup(0)
                if more_x:
                    normed = own.mark(norm_x(m * 2 + 4, 0))
                lo_step(par, m + 1)
                if more_x:
                    own.need(normed)
                    x_limited = own.mark(limit_x(0))
                limited = own.mark(limit_sup(m * 2 + 1, 1))
                if more_x:
                    own.need(x_limited)
                    round_x(0)
                if more_lo:
                    x_lo(m * 2 + 3, 1)
                own.need(limited)
                round_sup(1)
                if more_x:
                    link(norm_x(m * 2 + 5, 1))
                    link(limit_x(1))
                    round_x(1)

            for t in range(4):
                if t >= 2:
                    x_lo(t - 2, t % 2)
                link(norm_x(t, t % 2))
                link(limit_x(t % 2))
                round_x(t % 2)
            for m in range(LOOP0):
                pair(m, m % 2)
            with dve.Fori(0, TRIPS0) as j:
                own.enter(j, 2 * 6)
                for par in range(2):
                    pair(j * 2 + (LOOP0 + par), par)
                own.leave(TRIPS0)
            for m in range(LOOP0 + 2 * TRIPS0, STEPS):
                pair(m, m % 2)

            def split(n, par, ready):
                dve.wait_ge(split_hi[n], ready)
                dve.tensor_tensor(w_lo[:, n, par * C * D:(par + 1) * C * D], w_raw[:, n, par, :],
                                  w_hi[:, n, par * C * D:(par + 1) * C * D].bitcast(F32), ALU.subtract).then_inc(split_lo[n], 1)

            def add_gnn(t):
                dve.scalar_tensor_tensor(x_sb[:, t, :], acc_bank(t // TQ, t % TQ), small[:, 4:5], x_sb[:, t, :],
                                         ALU.mult, ALU.add).then_inc(acc_read, 1)

            def statistics(t):
                dve.wait_ge(acc_read, t + 1)
                link(dve.bn_stats(stats[:, t % 4, :], x_sb[:, t, :]))
                dve.bn_aggr(mv[:, t, :], stats[:, t % 4, :]).then_inc(mid_ok, 1)

            def add_br(t):
                dve.wait_ge(router_mm, t + 1)
                dve.tensor_tensor(logits[:, t, :], side_bank(t // TQ + 1, 2 + t % 2)[:, 0:E], br_sb[:, :],
                                  ALU.add).then_inc(logits_ok, 1)

            for q in range(1, QUARTERS):
                t0 = TQ * (q - 1)
                lo_step(0, STEPS * q + 1)
                dve.wait_ge(adj_mm, STEPS * q + 1)
                for t in range(t0, t0 + TQ):
                    add_gnn(t)
                statistics(t0)
                for jj in range(MID):
                    lo_step(1, STEPS * q + 2 * jj + 2)
                    lo_step(0, STEPS * q + 2 * jj + 3)
                    statistics(t0 + jj + 1)
                    add_br(t0 + jj)
                lo_step(1, STEPS * (q + 1))
                add_br(t0 + MID)
            dve.wait_ge(adj_mm, STEPS * QUARTERS + 1)
            for t in range(T - TQ, T):
                add_gnn(t)
            for t in range(T - TQ, T):
                statistics(t)
            split(0, 0, 1)
            for t in range(T - TQ, T):
                add_br(t)
            dve.wait_ge(small_in, 64)
            dve.wait_ge(logits_ok, T)

            def te(i):
                return rt[:, i, :].rearrange("p (t e) -> p t e", e=E)

            def et(i):
                return rt[:, i, :].rearrange("p (e t) -> p e t", t=T)

            def over_e(v):
                return v.unsqueeze(2).to_broadcast([P, T, E])

            def over_t(v):
                return v.unsqueeze(2).to_broadcast([P, E, T])

            def v16(i):
                return rv[:, i, 0:16]

            iota_e = const("iota_e").unsqueeze(1).to_broadcast([P, T, E])
            link(dve.tensor_reduce(v16(0), logits[:, :, :], AX_X, ALU.max))
            dve.tensor_tensor(te(0), logits[:, :, :], over_e(v16(0)), ALU.subtract).then_inc(exp_in, 1)
            dve.wait_ge(bias_in, 64)
            link(dve.tensor_copy(b_hi[:, :], b_raw[:, :]))
            for base in (0, 64):
                dve.tensor_copy(bias_sb[base:base + 32, :], b_hi[base:base + 32, :].bitcast(F32))
                ins = dve.tensor_tensor(bias_sb[base + 32:base + 64, :], b_raw[base + 32:base + 64, :],
                                        b_hi[base + 32:base + 64, :].bitcast(F32), ALU.subtract)
            ins.then_inc(bias_ok, 1)
            dve.wait_ge(exp_ok, 1)
            link(dve.tensor_reduce(v16(1), te(1), AX_X, ALU.add))
            link(dve.reciprocal(v16(2), v16(1)))
            link(dve.tensor_tensor(te(2), te(1), over_e(v16(2)), ALU.mult))
            def pick(p, cand, mask, top, low):
                link(dve.tensor_reduce(v16(top), te(p), AX_X, ALU.max))
                link(dve.tensor_tensor(te(cand), te(p), over_e(v16(top)), ALU.is_equal))
                link(dve.scalar_tensor_tensor(te(cand), te(cand), -64.0, iota_e, ALU.mult, ALU.add))
                link(dve.tensor_reduce(v16(low), te(cand), AX_X, ALU.min))
                link(dve.tensor_tensor(te(mask), te(cand), over_e(v16(low)), ALU.is_equal))

            pick(2, 3, 4, 3, 4)
            link(dve.scalar_tensor_tensor(te(5), te(4), -4.0, te(2), ALU.mult, ALU.add))
            pick(5, 3, 6, 5, 6)
            dve.tensor_tensor(et(7).rearrange("p e t -> p t e"), te(4), te(6), ALU.add).then_inc(picked, 1)
            link(dve.tensor_tensor(v16(10), v16(3), v16(5), ALU.add))
            link(dve.tensor_scalar(v16(10), v16(10), 1e-9, None, ALU.max))
            link(dve.reciprocal(v16(11), v16(10)))
            dve.tensor_tensor(rv[:, 7, 0:T], v16(3), v16(11), ALU.mult)
            link(dve.tensor_tensor(rv[:, 7, T:2 * T], v16(5), v16(11), ALU.mult))
            dve.wait_ge(ranks, 1)
            within = ps[:, 0, 0:E * T]
            totals = ps[:, 1, 0:E * T]
            link(dve.tensor_tensor_scan(rt[:, 8, :], const("scan_keep"), totals, 0.0, ALU.mult, ALU.add))
            link(dve.tensor_tensor(rt[:, 9, :], rt[:, 8, :], totals, ALU.subtract))
            link(dve.tensor_tensor(rt[:, 9, :], rt[:, 9, :], within, ALU.add))
            link(dve.tensor_tensor(te(10), et(8)[:, :, T - 1:T].to_broadcast([P, E, E]),
                                   const("full_tiles").unsqueeze(1).to_broadcast([P, E, E]), ALU.is_gt))
            link(dve.tensor_reduce(v16(12), te(10), AX_X, ALU.add))
            link(dve.tensor_scalar(v16(12), v16(12), 1.0, None, ALU.max))
            link(dve.tensor_tensor_scan(v16(13), const("ones")[:, 0:E], v16(12), 0.0, ALU.mult, ALU.add))
            link(dve.tensor_tensor(v16(13), v16(13), v16(12), ALU.subtract))
            link(dve.tensor_scalar(v16(14), v16(13), float(P), None, ALU.mult))
            link(dve.tensor_tensor(et(9), et(9), over_t(v16(14)), ALU.add))
            for k, mask in ((0, 4), (1, 6)):
                link(dve.tensor_tensor(te(11), te(mask), et(9).rearrange("p e t -> p t e"), ALU.mult))
                link(dve.tensor_reduce(rv[:, 15, k * T:(k + 1) * T], te(11), AX_X, ALU.add))
            pos = rv[:, 15, :]
            pos_i = rt[:, 12, 0:32].bitcast(I32)
            hi_i = rt[:, 12, 32:64].bitcast(I32)
            lo_i = rt[:, 12, 64:96].bitcast(I32)
            pos_slot = rt[:, 12, 96:128]
            link(dve.tensor_copy(pos_i, pos))
            link(dve.tensor_scalar(hi_i, pos_i, 7, None, ALU.arith_shift_right))
            link(dve.tensor_scalar(lo_i, pos_i, P - 1, None, ALU.bitwise_and))
            link(dve.tensor_copy(pos_slot, hi_i))
            link(dve.tensor_copy(pos_row, lo_i))
            link(dve.tensor_copy(rt[:, 13, 0:32].bitcast(F32R), rv[:, 7, :]))
            link(dve.tensor_tensor(rt[:, 13, 32:64], rv[:, 7, :], rt[:, 13, 0:32], ALU.subtract))
            for i in range(2):
                dve.wait_ge(mid_out[i], 16 * T)
            A = TOP * T
            link(dve.tensor_tensor(hit_slot[:, :].rearrange("p (a s) -> p a s", a=A),
                                   const("iota_slot").unsqueeze(1).to_broadcast([P, A, TAB]),
                                   pos_slot.unsqueeze(2).to_broadcast([P, A, TAB]), ALU.is_equal))
            for k in range(TOP):
                dve.tensor_tensor(hit_row[:, k * T:(k + 1) * T, :], const("iota_row").unsqueeze(1).to_broadcast([P, T, P]),
                                  pos_row[:, k * T:(k + 1) * T].unsqueeze(2).to_broadcast([P, T, P]), ALU.is_equal)
                half = hit_slot[:, k * T * TAB:(k + 1) * T * TAB]
                vals = [const("token_1"), rt[:, 13, k * T:(k + 1) * T], rt[:, 13, 32 + k * T:32 + (k + 1) * T]]
                for n, v in enumerate(vals):
                    ins = dve.tensor_tensor(hit_val[:, k, n, :].rearrange("p (a s) -> p a s", a=T),
                                            half.rearrange("p (a s) -> p a s", a=T),
                                            v.unsqueeze(2).to_broadcast([P, T, TAB]), ALU.mult)
                ins.then_inc(hits_ok, 1)
            slot_f = rt[:, 11, 0:TAB]
            started = rt[:, 0:4, :].rearrange("p a b -> p (a b)")[:, 0:TAB * E].rearrange("p (s e) -> p s e", e=E)
            link(dve.tensor_tensor(started, const("iota_slot").unsqueeze(2).to_broadcast([P, TAB, E]),
                                   v16(13).unsqueeze(1).to_broadcast([P, TAB, E]), ALU.is_ge))
            link(dve.tensor_reduce(slot_f, started, AX_X, ALU.add))
            link(dve.tensor_scalar(slot_f, slot_f, -1.0, None, ALU.add))
            link(dve.tensor_scalar(sel1_col[:, :], slot_f, const("is_bias1"), None, ALU.is_equal))
            link(dve.tensor_scalar(sel2_col[:, :], slot_f, const("is_bias2"), None, ALU.is_equal))
            new = rt[:, 11, 64:64 + TAB]
            not_last = rt[:, 11, 128:128 + TAB]
            link(dve.tensor_scalar(not_last, slot_f, float(E - 1), None, ALU.is_lt))
            link(dve.memset(new, 0.0))
            link(dve.tensor_tensor(new[:, 0:TAB - 1], slot_f[:, 1:TAB], slot_f[:, 0:TAB - 1], ALU.not_equal))
            link(dve.tensor_tensor(new[:, 0:TAB - 1], new[:, 0:TAB - 1], not_last[:, 1:TAB], ALU.mult))
            starts = rt[:, 12, 0:TAB]
            PAIRS = SLOTS // 2

            def first(v, n=PAIRS + 1):
                return v[:, 0:2 * n].rearrange("p (n two) -> p n two", two=2)[:, :, 0]

            def second(v, n=PAIRS + 1):
                return v[:, 0:2 * n].rearrange("p (n two) -> p n two", two=2)[:, :, 1]

            pair_e, pair_s = rt[:, 12, 64:64 + PAIRS + 1], rt[:, 12, 96:96 + PAIRS + 1]
            dve.memset(starts[:, 0:1], 1.0)
            link(dve.tensor_copy(starts[:, 1:TAB], new[:, 0:TAB - 1]))
            link(dve.scalar_tensor_tensor(pair_e, second(slot_f), 16.0, first(slot_f), ALU.mult, ALU.add))
            link(dve.scalar_tensor_tensor(pair_s, second(starts), 2.0, first(starts), ALU.mult, ALU.add))
            e_4, s_4 = rt[:, 12, 128:128 + PAIRS], rt[:, 12, 160:160 + PAIRS]
            link(dve.scalar_tensor_tensor(e_4, pair_e[:, 1:PAIRS + 1], 256.0, pair_e[:, 0:PAIRS], ALU.mult, ALU.add))
            link(dve.scalar_tensor_tensor(s_4, pair_s[:, 1:PAIRS + 1], 4.0, pair_s[:, 0:PAIRS], ALU.mult, ALU.add))
            link(dve.scalar_tensor_tensor(s_4, s_4, 65536.0, e_4, ALU.mult, ALU.add))
            link(dve.tensor_copy(plan[:, :], s_4))
            used = rt[:, 11, 192:193]
            link(dve.tensor_tensor(used, v16(13)[:, E - 1:E], v16(12)[:, E - 1:E], ALU.add))
            link(dve.tensor_scalar(used, used, 1.0, None, ALU.add))
            used_i = rt[:, 11, 193:194].bitcast(I32)
            link(dve.tensor_copy(used_i, used))
            link(dve.tensor_scalar(pairs[:, :], used_i, 1, None, ALU.arith_shift_right))
            split(0, 1, 2)
            dve.wait_ge(table_mm, 1)
            tab = ps[:, 2, 0:3 * TAB].rearrange("p (n s) -> p n s", n=3)
            dve.tensor_scalar(tok_i[:, :], tab[:, 0, :], -1.0, 0.0, ALU.add, ALU.max).then_inc(tok_ok, 1)
            link(dve.tensor_scalar(rt[:, 10, 0:TAB], tab[:, 0, :], 0.0, const("dump_row_1"), ALU.is_equal, ALU.mult))
            link(dve.scalar_tensor_tensor(scat_i[:, :], tab[:, 0, :], -1.0, rt[:, 10, 0:TAB], ALU.add, ALU.add))
            link(dve.tensor_copy(rt[:, 10, 128:128 + TAB], tab[:, 1, :]))
            dve.tensor_tensor(gate[:, 1:TAB + 1], rt[:, 10, 128:128 + TAB], tab[:, 2, :], ALU.add).then_inc(table_ok, 1)
            split(1, 0, 1)

            def slot_x_lo(s, par):
                dve.wait_ge(x_hi_ok, s + 1)
                dve.tensor_tensor(xt_lo[:, par, :], xt_ps(par), xt_hi[:, par, :].bitcast(F32), ALU.subtract).then_inc(x_lo_ok, 1)

            def slot_stats(s, par):
                dve.wait_ge(mm1, s + 1)
                link(dve.bn_stats(h_stats[:, par, :], h_ps(par)))
                dve.sem_inc(dve_turn, 1)
                dve.bn_aggr(h_mv[:, par, :], h_stats[:, par, :]).then_inc(h_var, 1)

            def split_next(n, e, start):
                with dve.If(start == 1):
                    at = bass.ds(((e + 1) & 1) * (C * D), C * D)
                    dve.wait_ge(split_hi[n], e + 2)
                    dve.tensor_tensor(w_lo[:, n, at], w_raw[:, n, :, :].rearrange("p a n -> p (a n)")[:, at],
                                      w_hi[:, n, at].bitcast(F32), ALU.subtract).then_inc(split_lo[n], 1)

            def gated(n, par):
                dve.wait_ge(mm2, n)
                dve.wait_ge(scattered, n * 16)
                dve.tensor_scalar(y_sb[:, par, :], y_ps(par), gate[:, bass.ds(n, 1)], None, ALU.mult).then_inc(y_ok, 1)

            word = load_plan(dve, 0)
            live = dve.value_load(pairs[0:1, 0:1], min_val=1, max_val=SLOTS // 2)
            slot_x_lo(0, 0)
            slot_x_lo(1, 1)
            slot_stats(0, 0)
            slot_x_lo(2, 0)
            slot_stats(1, 1)
            split_next(0, expert_in(word, 1), starts_in(word, 1))
            dve.sem_inc(y_ok, 2)
            with dve.Fori(0, SLOTS // 2) as j:
                with dve.If(j < live):
                    own.enter(j, 2)
                    for par in range(2):
                        s = j * 2 + par
                        dve.wait_ge(g_hi_ok, s + 1)
                        dve.tensor_tensor(gt_lo[:, par, :], g_sb[:, par, :], gt_hi[:, par, :].bitcast(F32),
                                          ALU.subtract).then_inc(g_lo_ok, 1)
                        if par == 0:
                            with dve.If(j > 0):
                                gated(s, 1)
                        else:
                            gated(s, 0)
                        slot_x_lo(s + 3, 1 - par)
                        slot_stats(s + 2, par)
                        if par == 0:
                            word = load_plan(dve, j)
                        split_next(0, expert_in(word, par + 2), starts_in(word, par + 2))
                        split_next(1, expert_in(word, par), starts_in(word, par))
                    own.leave(0)
            gated(live * 2, 1)

        @block.tensor
        def _(pe):
            ident = const("ident")
            ones = const("ones")
            pe.wait_ge(consts_in, 16)
            for i, col in ((0, 8), (1, 15)):
                pe.wait_ge(w_means, i + 1)
                pe.matmul(side_bank(0, i)[:, 0:1], ones, small[:, col:col + 1], start=True, stop=True).then_inc(w_sums, 1)

            def transpose_x(t, par):
                pe.wait_ge(xq_ready, t + 1)
                for c in range(C):
                    ins = pe.transpose(side_bank(0, par)[:, c * P:(c + 1) * P], xq[:, par, c * P:(c + 1) * P], ident)
                ins.then_inc(xq_t, 1)

            def support(t, par):
                pe.wait_ge(xq_lo_ok, t + 1)
                if not isinstance(t, int) or t >= 2:
                    pe.wait_ge(relu_ok, t - 1)
                for part in (xq_hi, xq_lo):
                    for c in range(C):
                        ins = pe.matmul(side_bank(0, 2 + par), part[:, par, c * P:(c + 1) * P],
                                        w_int[:, c * D:(c + 1) * D],
                                        start=part is xq_hi and c == 0, stop=part is xq_lo and c == C - 1)
                ins.then_inc(sup_mm, 1)

            sup_flat = sup[:, :, :].rearrange("p t d -> p (t d)")

            def step(q, m, par, n, first=False, last=False):
                pe.wait_ge(adj_lo_ok, n)
                for k in range(2):
                    for i in range(TQ):
                        for part in (adj_hi, adj_lo):
                            ins = pe.matmul(acc_bank(q, i), part[:, par, k, i * P:(i + 1) * P],
                                            sup_flat[:, bass.ds((m * 2 + k) * D, D)],
                                            start=first and k == 0 and part is adj_hi,
                                            stop=last and k == 1 and part is adj_lo)
                ins.then_inc(adj_mm, 1)

            pe.sem_inc(adj_mm, 1)
            pe.wait_ge(w_ready, 1)
            def pair(m, par):
                more = not (isinstance(m, int) and m == STEPS - 1)
                support(m * 2, 0)
                if more:
                    transpose_x(m * 2 + 2, 0)
                support(m * 2 + 1, 1)
                if more:
                    transpose_x(m * 2 + 3, 1)
                if not isinstance(m, int) or m >= 1:
                    pe.wait_ge(sup_ok, m * 2)
                    step(0, m - 1, 1 - par, m, first=isinstance(m, int) and m == 1)

            transpose_x(0, 0)
            transpose_x(1, 1)
            for m in range(LOOP0):
                pair(m, m % 2)
            with pe.Fori(0, TRIPS0) as j:
                for par in range(2):
                    pair(j * 2 + (LOOP0 + par), par)
            for m in range(LOOP0 + 2 * TRIPS0, STEPS):
                pair(m, m % 2)
            pe.wait_ge(sup_ok, T)
            step(0, STEPS - 1, 1, STEPS, last=True)

            def finish_t(t):
                pe.wait_ge(xn_ok, t + 1)
                if t >= 2:
                    pe.wait_ge(xn_t_ok, t - 1)
                for c in range(C):
                    ins = pe.transpose(side_bank(t // TQ + 1, t % 2)[:, c * P:(c + 1) * P],
                                       xn[:, t % 2, c * P:(c + 1) * P], ident)
                ins.then_inc(xn_tp, 1)

            def router(t):
                pe.wait_ge(xn_t_ok, t + 1)
                if t >= 2:
                    pe.wait_ge(logits_ok, t - 1)
                for c in range(C):
                    ins = pe.matmul(side_bank(t // TQ + 1, 2 + t % 2)[:, 0:E], xn_t[:, t % 2, c * P:(c + 1) * P],
                                    wr_sb[:, c * E:(c + 1) * E], start=c == 0, stop=c == C - 1)
                ins.then_inc(router_mm, 1)

            pe.wait_ge(small_in, 64)
            for q in range(1, QUARTERS):
                t0 = TQ * (q - 1)
                if q > 1:
                    pe.wait_ge(logits_ok, t0)
                n = STEPS * q + 1
                step(q, 0, 0, n, first=True)
                for jj in range(MID):
                    if jj == 0:
                        pe.wait_ge(acc_read, t0 + TQ)
                    finish_t(t0 + jj)
                    step(q, 2 * jj + 1, 1, n + 2 * jj + 1)
                    router(t0 + jj)
                    step(q, 2 * jj + 2, 0, n + 2 * jj + 2)
                finish_t(t0 + MID)
                step(q, STEPS - 1, 1, STEPS * (q + 1), last=True)
                router(t0 + MID)
            pe.wait_ge(acc_read, T)
            for t in range(T - TQ, T):
                finish_t(t)
                if t > T - TQ:
                    router(t - 1)
            router(T - 1)

            pe.wait_ge(picked, 1)
            chosen = rt[:, 7, :]
            pe.matmul(ps[:, 0, 0:E * T], const("tri"), chosen, start=True, stop=True)
            pe.matmul(ps[:, 1, 0:E * T], ones, chosen, start=True, stop=True).then_inc(ranks, 1)
            for k in range(TOP):
                pe.wait_ge(hits_ok, k + 1)
                for t in range(T):
                    ins = pe.matmul(ps[:, 2, 0:3 * TAB].rearrange("p (n s) -> p n s", n=3), hit_row[:, k * T + t, :],
                                    hit_val[:, k, :, t * TAB:(t + 1) * TAB],
                                    start=k == 0 and t == 0, stop=k == TOP - 1 and t == T - 1)
            ins.then_inc(table_mm, 1)

            def rows_t(s, par, landed):
                pe.wait_ge(gathered[par], landed)
                for c in range(C):
                    ins = pe.transpose(xt_ps(par)[:, c * P:(c + 1) * P], xg[:, par, c * P:(c + 1) * P], ident)
                ins.then_inc(x_tp, 1)

            def layer(dst, n, par, e, act_hi, act_lo, sel, done):
                pe.matmul(dst, sel[:, par, :], bias_sb[:, :], start=True, stop=False)
                for c in range(C):
                    at = bass.ds((e & 1) * (C * D) + c * D, D)
                    pe.matmul(dst, act_hi[:, par, c * P:(c + 1) * P], w_hi[:, n, at], start=False, stop=False)
                    pe.matmul(dst, act_lo[:, par, c * P:(c + 1) * P], w_hi[:, n, at], start=False, stop=False)
                    ins = pe.matmul(dst, act_hi[:, par, c * P:(c + 1) * P], w_lo[:, n, at], start=False, stop=c == C - 1)
                ins.then_inc(done, 1)

            pe.wait_ge(table_ok, 1)
            rows_t(0, 0, 16)
            rows_t(1, 1, 16)
            e_1 = expert_in(load_plan(pe, 0), 1)
            live = pe.value_load(pairs[0:1, 0:1], min_val=1, max_val=SLOTS // 2)
            pe.wait_ge(x_lo_ok, 1)
            pe.wait_ge(split_lo[0], 1)
            pe.wait_ge(sel_ok, 3)
            pe.wait_ge(bias_ok, 1)
            layer(h_ps(0), 0, 0, 0, xt_hi, xt_lo, sel1, mm1)
            rows_t(2, 0, 32)
            pe.wait_ge(x_lo_ok, 2)
            pe.wait_ge(split_lo[0], e_1 + 1)
            layer(h_ps(1), 0, 1, e_1, xt_hi, xt_lo, sel1, mm1)
            with pe.Fori(0, SLOTS // 2) as j:
                with pe.If(j < live):
                    for par in range(2):
                        s = j * 2 + par
                        pe.wait_ge(h_hat_ok, s + 1)
                        for c in range(C):
                            ins = pe.transpose(ht_ps(par)[:, c * P:(c + 1) * P], h_hat[:, par, c * P:(c + 1) * P], ident)
                        ins.then_inc(h_tp, 1)
                        rows_t(s + 3, 1 - par, j * 16 + (32 + 16 * par))
                        if par == 0:
                            word = load_plan(pe, j)
                        e_s, e_a = expert_in(word, par), expert_in(word, par + 2)
                        pe.wait_ge(x_lo_ok, s + 3)
                        pe.wait_ge(split_lo[0], e_a + 1)
                        pe.wait_ge(sel_ok, s * 2 + 4)
                        layer(h_ps(par), 0, par, e_a, xt_hi, xt_lo, sel1, mm1)
                        pe.wait_ge(g_lo_ok, s + 1)
                        pe.wait_ge(split_lo[1], e_s + 1)
                        pe.wait_ge(y_ok, s + 1)
                        layer(y_ps(par), 1, par, e_s, gt_hi, gt_lo, sel2, mm2)


_OUT_ROWS = N + P


def kernel(x, adj, L0_gnn_adj_scaling_factor, L0_gnn_weight, L0_gnn_wgt_alpha, L0_gnn_act_alpha, L0_gnn_act_alpha2,
           L0_ffn_Wr, L0_ffn_br, L0_ffn_W1, L0_ffn_b1, L0_ffn_g1, L0_ffn_be1, L0_ffn_W2, L0_ffn_b2):
    import concourse.bacc as bacc
    from concourse.bass_utils import run_bass_kernel_spmd

    def chunked(w):
        w = np.asarray(w)
        w = w.reshape(-1, C, P, w.shape[-1]).transpose(0, 2, 1, 3)
        return np.ascontiguousarray(w.reshape(-1, C * w.shape[-1]))

    def rows(v):
        return np.ascontiguousarray(np.broadcast_to(v, (P, v.size)))

    scalars = np.stack([np.asarray(v).reshape(()) for v in
                        (L0_gnn_adj_scaling_factor, L0_gnn_wgt_alpha, L0_gnn_act_alpha, L0_gnn_act_alpha2)])
    by_hidden = [np.ascontiguousarray(np.asarray(v).reshape(E * C, P).T) for v in (L0_ffn_g1, L0_ffn_be1)]
    ins = {
        "x": np.asarray(x),
        "adj_t": np.ascontiguousarray(np.asarray(adj).T),
        "gnn_w": chunked(L0_gnn_weight),
        "scalars": rows(scalars),
        "wr": chunked(L0_ffn_Wr),
        "br": rows(np.asarray(L0_ffn_br)),
        "w1": chunked(L0_ffn_W1),
        "b1": np.asarray(L0_ffn_b1),
        "g1": by_hidden[0],
        "be1": by_hidden[1],
        "w2": chunked(L0_ffn_W2),
        "b2": np.asarray(L0_ffn_b2),
        "consts": constants(),
    }
    nc = bacc.Bacc("TRN2", target_bir_lowering=False, num_devices=1)
    aps = {n: nc.dram_tensor(f"in_{n}", a.shape, mybir.dt.from_np(a.dtype), kind="ExternalInput").ap()
           for n, a in ins.items()}
    xn_rows = nc.dram_tensor("xn_rows", [N, D], F32, kind="Internal").ap()
    out = nc.dram_tensor("out", [_OUT_ROWS, D], F32, kind="ExternalOutput").ap()
    gnn_moe_program(nc, xn_rows=xn_rows, out=out, **aps)
    r = run_bass_kernel_spmd(nc, [{f"in_{n}": a for n, a in ins.items()}], core_ids=[0])
    return r.results[0]["out"][:N]
```
